# Optimizing a Trainium2 kernel written in Bass

```python
import numpy as np
import jax
import jax.numpy as jnp

def _softmax(x, axis=-1):
    return jax.nn.softmax(x, axis=axis)

def _gelu(x):
    return jax.nn.gelu(x, approximate=True)

def _silu(x):
    return jax.nn.silu(x)

def _sigmoid(x):
    return jax.nn.sigmoid(x)

def _layernorm(x, axis=-1, eps=1e-05):
    m = jnp.mean(x, axis=axis, keepdims=True)
    v = jnp.var(x, axis=axis, keepdims=True)
    return (x - m) / jnp.sqrt(v + eps)

def _scatter_add(tgt, idx, src, axis=0):
    return tgt.at[idx].add(src)

def _segment_sum(src, seg, n):
    return jax.ops.segment_sum(src, seg, n)
kernel_name = 'mk_conv_preact_d1_conv_nchw384_r4_08fc31'

def setup_inputs(seed: int=0):
    np.random.seed(seed)
    _w = jnp.asarray

    def _rec_inputs():
        import jax
        import jax.numpy as jnp
        _gk = jax.random.key(seed)
        x = -0.0002221 + 1 * jax.random.normal(jax.random.fold_in(_gk, 1), (16, 96, 16, 16), jnp.float32)
        return x
    x = _rec_inputs()

    def _L0_conv_setup():
        import jax, jax.numpy as jnp
        import numpy as np
        BANDLIMIT = 0.5
        STEP_SCALE = 1.0
        LN_EPS = 1e-05

        def _layernorm(x, g, b):
            mu = jnp.mean(x, axis=-1, keepdims=True)
            xc = x - mu
            inv = jax.lax.rsqrt(jnp.mean(xc * xc, axis=-1, keepdims=True) + LN_EPS)
            return xc * inv * g + b
        key = jax.random.key(seed)
        ks = jax.random.split(key, 12)
        B, C, H, W = (16, 96, 16, 16)
        P = 48
        x = jax.random.normal(ks[0], (B, C, H, W), dtype=jnp.float32)
        ln1_g = 1.0 + 0.1 * jax.random.normal(ks[1], (C,), dtype=jnp.float32)
        ln1_b = 0.1 * jax.random.normal(ks[2], (C,), dtype=jnp.float32)
        lam_re = -(0.3 + jax.random.uniform(ks[3], (P,), dtype=jnp.float32))
        lam_im = jnp.pi * jnp.arange(P, dtype=jnp.float32)
        Lambda = jnp.stack([lam_re, lam_im], axis=-1)
        Bmat = jax.random.normal(ks[4], (P, C, 2), dtype=jnp.float32) / np.sqrt(C)
        Cmat = jax.random.normal(ks[5], (C, P, 2), dtype=jnp.float32) / np.sqrt(P)
        D = jax.random.normal(ks[6], (C,), dtype=jnp.float32)
        log_step = jax.random.uniform(ks[7], (P,), dtype=jnp.float32, minval=float(np.log(0.001)), maxval=float(np.log(0.1)))
        ln2_g = 1.0 + 0.1 * jax.random.normal(ks[8], (C,), dtype=jnp.float32)
        ln2_b = 0.1 * jax.random.normal(ks[9], (C,), dtype=jnp.float32)
        W_enc = jax.random.normal(ks[10], (2 * C, C), dtype=jnp.float32) / np.sqrt(C)
        W_dec = jax.random.normal(ks[11], (C, C), dtype=jnp.float32) / np.sqrt(C)
        return {'x': x, 'ln1_g': ln1_g, 'ln1_b': ln1_b, 'Lambda': Lambda, 'Bmat': Bmat, 'Cmat': Cmat, 'D': D, 'log_step': log_step, 'ln2_g': ln2_g, 'ln2_b': ln2_b, 'W_enc': W_enc, 'W_dec': W_dec}
    _L0_conv_all = _L0_conv_setup()
    _L0_conv_in = {k: v for k, v in _L0_conv_all.items() if k in ('ln1_g', 'ln1_b', 'Lambda', 'Bmat', 'Cmat', 'D', 'log_step', 'ln2_g', 'ln2_b', 'W_enc', 'W_dec')}
    del _L0_conv_all
    return {'x': x, 'L0_conv_ln1_g': _L0_conv_in['ln1_g'], 'L0_conv_ln1_b': _L0_conv_in['ln1_b'], 'L0_conv_Lambda': _L0_conv_in['Lambda'], 'L0_conv_Bmat': _L0_conv_in['Bmat'], 'L0_conv_Cmat': _L0_conv_in['Cmat'], 'L0_conv_D': _L0_conv_in['D'], 'L0_conv_log_step': _L0_conv_in['log_step'], 'L0_conv_ln2_g': _L0_conv_in['ln2_g'], 'L0_conv_ln2_b': _L0_conv_in['ln2_b'], 'L0_conv_W_enc': _L0_conv_in['W_enc'], 'L0_conv_W_dec': _L0_conv_in['W_dec']}

def reference(x, L0_conv_ln1_g, L0_conv_ln1_b, L0_conv_Lambda, L0_conv_Bmat, L0_conv_Cmat, L0_conv_D, L0_conv_log_step, L0_conv_ln2_g, L0_conv_ln2_b, L0_conv_W_enc, L0_conv_W_dec):
    import jax
    import jax.numpy as jnp

    def _L0_conv_ref(x, ln1_g, ln1_b, Lambda, Bmat, Cmat, D, log_step, ln2_g, ln2_b, W_enc, W_dec):
        import jax, jax.numpy as jnp
        import numpy as np
        BANDLIMIT = 0.5
        STEP_SCALE = 1.0
        LN_EPS = 1e-05

        def _layernorm(x, g, b):
            mu = jnp.mean(x, axis=-1, keepdims=True)
            xc = x - mu
            inv = jax.lax.rsqrt(jnp.mean(xc * xc, axis=-1, keepdims=True) + LN_EPS)
            return xc * inv * g + b
        Bsz, C, H, W = x.shape
        u = x.reshape(Bsz, C, H * W).transpose(0, 2, 1)
        fx = _layernorm(u, ln1_g, ln1_b)
        res = fx
        lam = Lambda[..., 0] + 1j * Lambda[..., 1]
        Bc = Bmat[..., 0] + 1j * Bmat[..., 1]
        Cc = Cmat[..., 0] + 1j * Cmat[..., 1]
        step = STEP_SCALE * jnp.exp(log_step)
        freqs = step / STEP_SCALE * jnp.abs(Lambda[..., 1]) / (2.0 * jnp.pi)
        mask = (freqs < BANDLIMIT * 0.5).astype(Cc.dtype)
        Cc = Cc * mask
        lam_bar = jnp.exp(lam * step)
        B_bar = ((lam_bar - 1.0) / lam)[:, None] * Bc
        Bu = jnp.einsum('ph,blh->blp', B_bar, fx.astype(B_bar.dtype))
        lam_el = jnp.broadcast_to(lam_bar, Bu.shape)

        def binop(a, b):
            return (a[0] * b[0], b[0] * a[1] + b[1])
        _, xs = jax.lax.associative_scan(binop, (lam_el, Bu), axis=1)
        y = 2.0 * jnp.real(jnp.einsum('hp,blp->blh', Cc, xs)) + D * fx
        y = jax.nn.gelu(y, approximate=False) + res
        fy = _layernorm(y, ln2_g, ln2_b)
        z = fy @ W_enc.T
        z1, z2 = jnp.split(z, 2, axis=-1)
        z = z1 * jax.nn.gelu(z2, approximate=False)
        y = z @ W_dec.T + fy
        return y.transpose(0, 2, 1).reshape(Bsz, C, H, W)

    def _gn(v, G=32, eps=1e-05):
        B_, C_, H_, W_ = v.shape
        g = v.reshape(B_, G, C_ // G, H_, W_)
        m = jnp.mean(g, axis=(2, 3, 4), keepdims=True)
        s = jnp.var(g, axis=(2, 3, 4), keepdims=True)
        return ((g - m) / jnp.sqrt(s + eps)).reshape(v.shape)

    def _ln_c(v, eps=1e-06):
        m = jnp.mean(v, axis=1, keepdims=True)
        s = jnp.var(v, axis=1, keepdims=True)
        return (v - m) / jnp.sqrt(s + eps)

    def _ln_t(v, eps=1e-05):
        m = jnp.mean(v, axis=-1, keepdims=True)
        s = jnp.var(v, axis=-1, keepdims=True)
        return (v - m) / jnp.sqrt(s + eps)

    def _to_tokens(v):
        B_, C_, H_, W_ = v.shape
        return v.reshape(B_, C_, H_ * W_).transpose(0, 2, 1)

    def _from_tokens(t, like):
        B_, C_, H_, W_ = like.shape
        return t.transpose(0, 2, 1).reshape(B_, C_, H_, W_)
    x = x + _L0_conv_ref(_gn(x), L0_conv_ln1_g, L0_conv_ln1_b, L0_conv_Lambda, L0_conv_Bmat, L0_conv_Cmat, L0_conv_D, L0_conv_log_step, L0_conv_ln2_g, L0_conv_ln2_b, L0_conv_W_enc, L0_conv_W_dec)
    return x

_drawn_inputs = setup_inputs


def setup_inputs(seed=0):
    import zlib

    import numpy as np

    out = dict(_drawn_inputs(seed))
    spreads = {}
    factors = {}
    for name, (base, spread) in spreads.items():
        noise = np.random.default_rng([zlib.crc32(name.encode()), seed]).standard_normal(out[name].shape)
        drawn = base * np.exp(spread * noise) if base else spread * noise
        out[name] = jnp.asarray(drawn.astype(out[name].dtype))
    for name, factor in factors.items():
        out[name] = (out[name] * factor).astype(out[name].dtype)
    return out
```

```python
from contextlib import ExitStack

import concourse.bass as bass
from concourse import mybir
import numpy as np

ALU = mybir.AluOpType
ACT = mybir.ActivationFunctionType
F32 = mybir.dt.float32
BF16 = mybir.dt.bfloat16
I32 = mybir.dt.int32

B, C, L = 16, 96, 256
P2 = 96
T = 8
NA = L // T
HB = B // 2
HC = HB * L
RC = HB * NA
TILE = 512
NT = HC // TILE
RT = TILE // RC
CH = 128
NCH = HC // CH
SR = 80
GROUP = 3
NGRP = GROUP * L
GN_EPS = 1e-5
LN_EPS = 1e-5

POWERS = list(range(T + 1)) + [2 * T - 1, 2 * T, 4 * T, 8 * T, 16 * T]
NK = len(POWERS)
K15 = POWERS.index(2 * T - 1)
NX = 6
TWO_PI_HI = 6.28125
TWO_PI_MID = 0.0019340515136718750
TWO_PI_LO = 2 * np.pi - TWO_PI_HI - TWO_PI_MID
PI_BELOW = 3.1415925
ROUND = 1.5 * 2.0 ** 23
RSQRT_SEED = float(0x5F1FFFF9)

(LR, LI, LS, RHO, NRHO, G1, B1, DD, G2, B2, KV) = range(11)
NS = KV + NK
(M_GM, M_GV, M_P, M_ID, M_SW, M_B, M_BS, M_C, M_CS, M_B1, M_WD, M_WE) = [96 * i for i in range(12)]
M_Z = M_WE + 192
ZW = 2 * 15 + 65
NM = M_Z + ZW
N_EARLY = M_ID


def s5_block(nc, x, small, mats, mask_in, out):
    ctx = ExitStack()
    with ctx:
        def sb(name, shape, dt=F32):
            return ctx.enter_context(nc.sbuf_tensor(name, shape, dt))

        def sem(name):
            return ctx.enter_context(nc.semaphore(name))

        xs = sb("xs", [C, B, L])
        h = sb("h", [C, 2, HC])
        xc = sb("xc", [C, 2, HC])
        sq = sb("sq", [C, 2, HC])
        fx = sb("fx", [C + 1, 2, HC])
        w = sb("w", [P2, 2, HC])
        y2 = sb("y2", [C, 2, HC])
        fy = sb("fy", [C, 2, HC])
        res = sb("res", [C, 2, HC])
        X = sb("X", [P2, 2, HB, NA + 1])
        gl, zz, gz = h, w, y2
        ost = xc

        sm = sb("sm", [96, NS])
        mt = sb("mt", [96, NM])
        rotT = sb("rotT", [96, 2, T, 96])
        rotX = sb("rotX", [96, 2, NX, 96])
        bst = sb("bst", [96, C + 1])
        bt1 = sb("bt1", [96, C])
        um = sb("um", [C + 1, T, 96])
        yl = sb("yl", [96, 2, T, 96])
        yc = sb("yc", [96, 2, T, 96])
        dm = sb("dm", [96, 96])
        bcm = sb("bcm", [SR, NCH, 96], BF16)
        bcmask = sb("bcmask", [SR, NCH])
        be = sb("be", [96, 2])
        db = sb("db", [96, 1])
        tb = sb("tb", [96, 24, NK])
        sc = sb("sc", [96, 40])
        st = sb("st", [C, B, 6])
        gn = sb("gn", [C, 2, 8, 16])
        rs = sb("rs", [SR, 2, 6, CH])
        spl = sb("spl", [SR, 2, CH], BF16)

        ps = ctx.enter_context(nc.psum_tensor("ps", [128, 8, TILE], F32))

        in_small, in_early, in_mats, in_mask = sem("in_small"), sem("in_early"), sem("in_mats"), sem("in_mask")
        in_x = [sem(f"in_x{k}") for k in range(4)]
        vec_chain = sem("vec_chain")
        pool_chain = sem("pool_chain")
        act_chain = sem("act_chain")
        angles_ready = sem("angles_ready")
        sines_ready = sem("sines_ready")
        tables_ready = sem("tables_ready")
        bst_ready = sem("bst_ready")
        rot_ready = sem("rot_ready")
        umat_done = sem("umat_done")
        um_ready = sem("um_ready")
        ymat_ready = sem("ymat_ready")
        bcm_ready = sem("bcm_ready")
        be_done = sem("be_done")
        be_ready = sem("be_ready")
        ones_ready = sem("ones_ready")
        gn_stats = sem("gn_stats")
        gn_mean = sem("gn_mean")
        gn_dev = sem("gn_dev")
        gn_var = sem("gn_var")
        gn_scale = sem("gn_scale")
        h_act, h_vec = sem("h_act"), sem("h_vec")
        centered = [sem("centered1"), sem("centered2")]
        squared = [sem("squared1"), sem("squared2")]
        variance = [sem("variance1"), sem("variance2")]
        inv_ready = [sem("inv_ready1"), sem("inv_ready2")]
        inv_bcast = [sem("inv_bcast1"), sem("inv_bcast2")]
        fx_ready, fy_ready = sem("fx_ready"), sem("fy_ready")
        u_done = sem("u_done")
        w_first = sem("w_first")
        w_ready = [sem("w_ready_a"), sem("w_ready_b")]
        x_sum = sem("x_sum")
        x_seed = sem("x_seed")
        x_ready = sem("x_ready")
        y_done = sem("y_done")
        gl_ready = sem("gl_ready")
        y2_ready = sem("y2_ready")
        z_done = sem("z_done")
        gz_ready = sem("gz_ready")
        zz_ready = sem("zz_ready")
        dec_done = sem("dec_done")
        res_ready = sem("res_ready")
        out_ready = sem("out_ready")
        stored = sem("stored")

        def bank(H, i):
            return ps[:, 4 * H + i, :]

        def cols(t, H, i, p=96):
            return t[0:p, H, TILE * i:TILE * (i + 1)]

        def rcols(t, H, b, p=96):
            return t[0:p, H, RC * b:RC * (b + 1)]

        def s(c, n=1):
            return sm[:, c:c + n]

        def m(c, n=96):
            return mt[:, c:c + n]

        def tbl(k, n=NK, at=0):
            return tb[:, k, at:at + n]

        block = ctx.enter_context(nc.Block())

        (ANG, XK, NRND, RED, EXM, TMP, SIN, SH, COS, SSG, NSS, RK, CM, SMG, CU, SU, CV, SV, XCO, XSI,
         AUX, AUX2, AUX3, AUX4) = range(24)
        (STEP, TH, RE, T1, T2, T3, CRE, CIM, DEN, AR, MASK, MR, MI, ABSI, T4, T5) = range(16)

        def scol(k):
            return sc[:, k:k + 1]

        @block.sync
        def _(sp):
            sp.dma_start(sm[:, :], small).then_inc(in_small, 16)
            for k in range(2):
                sp.dma_start(xs[:, 4 * k:4 * k + 4, :], x[:, 4 * k:4 * k + 4, :]).then_inc(in_x[k], 16)
            sp.dma_start(mt[:, N_EARLY:], mats[:, N_EARLY:]).then_inc(in_mats, 16)
            for k in range(2, 4):
                sp.dma_start(xs[:, 4 * k:4 * k + 4, :], x[:, 4 * k:4 * k + 4, :]).then_inc(in_x[k], 16)
            for H in range(2):
                sp.wait_ge(out_ready, T * (H + 1))
                sp.dma_start(out[:, HB * H:HB * (H + 1), :],
                             ost[:, H, :].rearrange("c (n l) -> c n l", l=L)).then_inc(stored, 16)
            sp.wait_ge(stored, 32)

        @block.gpsimd
        def _(pool):
            n = [0]

            def chain(ins):
                n[0] += 1
                ins.then_inc(pool_chain, 1)

            def settle():
                pool.wait_ge(pool_chain, n[0])

            nc.gpsimd.memset(fx[96:97, :, :], 1.0).then_inc(ones_ready, 1)
            nc.gpsimd.memset(X[:, :, :, 0:1], 0.0).then_inc(ones_ready, 1)
            pool.wait_ge(in_mats, 16)

            def combine(dst, mat_a, ca, mat_b, cb, n_mats):
                def mat(c):
                    return m(c).unsqueeze(1).broadcast_to([96, n_mats, 96])

                def coef(c):
                    return c.unsqueeze(2).broadcast_to([96, n_mats, 96])

                chain(nc.gpsimd.tensor_tensor(dst[:, 0], mat(mat_a), coef(ca), ALU.mult))
                chain(nc.gpsimd.tensor_tensor(dst[:, 1], mat(mat_b), coef(cb), ALU.mult))
                settle()
                return nc.gpsimd.tensor_tensor(dst[:, 0], dst[:, 0], dst[:, 1], ALU.add)

            pool.wait_ge(tables_ready, 1)
            combine(rotT, M_ID, tbl(COS, T), M_SW, tbl(NSS, T), T).then_inc(rot_ready, 1)
            combine(rotX, M_ID, tbl(XCO, NX), M_SW, tbl(XSI, NX), NX).then_inc(rot_ready, 1)
            combine(yl, M_C, tbl(CU, T), M_CS, tbl(SU, T), T).then_inc(ymat_ready, 1)
            combine(yc, M_C, tbl(CV, T), M_CS, tbl(SV, T), T).then_inc(ymat_ready, 1)
            for H in range(2):
                for i in range(NT):
                    pool.wait_ge(fy_ready, NT * H + i + 1)
                    xt = xs[:, HB * H:HB * (H + 1), :].rearrange("c n (a b) -> c b (n a)", b=T)
                    nc.gpsimd.tensor_tensor(
                        cols(res, H, i).rearrange("c (b m) -> c b m", b=RT),
                        cols(fy, H, i).rearrange("c (b m) -> c b m", b=RT),
                        xt[:, RT * i:RT * (i + 1), :], ALU.add).then_inc(res_ready, 1)

        @block.scalar
        def _(act):
            act.dma_start(mt[:, 0:N_EARLY], mats[:, 0:N_EARLY]).then_inc(in_early, 16)
            act.dma_start(bcmask[:, :], mask_in).then_inc(in_mask, 16)
            act.wait_ge(angles_ready, 1)
            nc.scalar.activation(tbl(SIN), tbl(RED), ACT.Sin).then_inc(sines_ready, 1)
            nc.scalar.activation(tbl(SH), tbl(RED), ACT.Sin, scale=0.5).then_inc(sines_ready, 1)

            def normalise(H, first, last):
                act.wait_ge(gn_scale, H + 1)
                hv = h[:, H, :].rearrange("c (b n a) -> c n b a", b=T, n=HB)
                for n in range(first, last):
                    nc.scalar.activation(
                        hv[:, n], xs[:, HB * H + n, :].rearrange("c (a b) -> c b a", b=T), ACT.Identity,
                        bias=gn[:, H, 6, n:n + 1], scale=gn[:, H, 5, n:n + 1]).then_inc(h_act, 1)

            def evacuate(k, H):
                for i in range(NT):
                    act.wait_ge(centered[k], NT * H + i + 1)
                    nc.scalar.activation(cols(sq, H, i), bank(H, i)[0:96, :], ACT.Square).then_inc(squared[k], 1)
                    nc.scalar.activation(cols(xc, H, i), bank(H, i)[0:96, :], ACT.Copy).then_inc(squared[k], 1)

            def first_state(H):
                act.wait_ge(u_done, NT * H + 1)
                nc.scalar.activation(rcols(w, H, 0), bank(H, 0)[0:96, 0:RC], ACT.Copy).then_inc(w_first, 1)

            def seed(H):
                act.wait_ge(x_sum, 5 * H + 1)
                act.wait_ge(ones_ready, 2)
                nc.scalar.activation(X[:, H, :, 1:], bank(H, 0)[0:96, 0:RC].rearrange("p (n a) -> p n a", a=NA),
                                     ACT.Copy).then_inc(x_seed, 1)

            def gelu_y(H):
                for i in range(NT):
                    act.wait_ge(y_done, NT * H + i + 1)
                    nc.scalar.activation(cols(gl, H, i), bank(H, i)[0:96, :], ACT.Gelu,
                                         bias=db[:, 0:1]).then_inc(gl_ready, 1)

            def gelu_z(H, i):
                act.wait_ge(z_done, NT * H + i + 1)
                nc.scalar.activation(cols(gz, H, i), bank(H, 2 * (i % 2) + 1)[0:96, :], ACT.Gelu,
                                     bias=be[:, 1:2]).then_inc(gz_ready, 1)

            act.wait_ge(in_mask, 16)
            nc.scalar.activation(bcm[:, :, :], bcmask[:, :].unsqueeze(2).broadcast_to([SR, NCH, 96]),
                                 ACT.Copy).then_inc(bcm_ready, 1)
            normalise(0, 0, HB // 2)
            evacuate(0, 0)
            normalise(1, 0, HB)
            evacuate(0, 1)
            act.wait_ge(be_done, 1)
            nc.scalar.activation(be[:, :], bank(1, 1)[0:96, 0:2], ACT.Copy).then_inc(be_ready, 1)
            act.wait_ge(umat_done, 1)
            nc.scalar.activation(um[:, 0:5, :], bank(1, 2)[0:97, 0:480].rearrange("c (b j) -> c b j", j=96),
                                 ACT.Copy).then_inc(um_ready, 1)
            nc.scalar.activation(um[:, 5:8, :], bank(1, 3)[0:97, 0:288].rearrange("c (b j) -> c b j", j=96),
                                 ACT.Copy).then_inc(um_ready, 1)
            first_state(0)
            first_state(1)
            seed(0)
            seed(1)
            gelu_y(0)
            evacuate(1, 0)
            gelu_y(1)
            evacuate(1, 1)
            for H in range(2):
                for i in range(NT):
                    gelu_z(H, i)

        @block.tensor
        def _(pe):
            def mm(o, lhsT, rhs, start=True, stop=True):
                return nc.tensor.matmul(o, lhsT, rhs, start=start, stop=stop)

            def group_norm(H):
                pe.wait_ge(gn_stats, HB * (H + 1))
                g = st[:, HB * H:HB * (H + 1), :]
                mm(bank(H, 0)[0:96, 0:HB], m(M_GM), g[:, :, 1], stop=False)
                mm(bank(H, 0)[0:96, 0:HB], m(M_GM), g[:, :, 4], start=False).then_inc(gn_mean, 1)
                pe.wait_ge(gn_dev, H + 1)
                mm(bank(H, 1)[0:96, 0:HB], m(M_GV), gn[:, H, 3, 0:HB]).then_inc(gn_var, 1)

            def center(k, H, src, waits):
                for i in range(NT):
                    waits(i)
                    mm(bank(H, i)[0:96, :], m(M_P), cols(src, H, i)).then_inc(centered[k], 1)

            def variances(k, H):
                for r in range(NCH):
                    if r % (TILE // CH) == 0:
                        pe.wait_ge(squared[k], 2 * (NT * H + r // (TILE // CH) + 1))
                    z = m(M_Z + 15 - r, SR)
                    last = mm(bank(H, 0)[0:SR, 0:CH], z, sq[:, H, CH * r:CH * (r + 1)],
                              start=(r == 0), stop=(r == NCH - 1))
                last.then_inc(variance[k], 1)

            def broadcast(k, H):
                pe.wait_ge(inv_ready[k], H + 1)
                pe.wait_ge(bcm_ready, 1)
                for i in range(NT):
                    for j in range(TILE // CH):
                        last = mm(bank(H, i)[0:96, CH * j:CH * (j + 1)], bcm[:, TILE // CH * i + j, :], spl[:, H, :])
                    last.then_inc(inv_bcast[k], 1)

            def inputs(H):
                pe.wait_ge(um_ready, 2)
                pe.wait_ge(ones_ready, 1)
                for i in range(NT):
                    pe.wait_ge(fx_ready, NT * H + i + 1)
                    for j in range(RT):
                        b = RT * i + j
                        last = mm(bank(H, i)[0:96, RC * j:RC * (j + 1)], um[:, b, :], rcols(fx, H, b, 97))
                    last.then_inc(u_done, 1)

            def seed_sum(H):
                pe.wait_ge(w_ready[H], T - 1)
                pe.wait_ge(rot_ready, 2)
                w7 = rcols(w, H, T - 1).rearrange("p (n a) -> p n a", a=NA)
                o = bank(H, 0)[0:96, 0:RC].rearrange("p (n a) -> p n a", a=NA)
                mm(o, rotX[:, 0, 0, :], w7, stop=False)
                mm(o[:, :, 1:], rotX[:, 0, 1, :], w7[:, :, 0:NA - 1], start=False).then_inc(x_sum, 1)

            def doubling(H, k):
                d = 2 ** (k + 1)
                pe.wait_ge(x_seed, H + 1)
                if k:
                    pe.wait_ge(x_ready, 4 * H + k)
                o = bank(H, 0)[0:96, 0:RC].rearrange("p (n a) -> p n a", a=NA)
                mm(o[:, :, d:], rotX[:, 0, 2 + k, :], X[:, H, :, 1:NA + 1 - d]).then_inc(x_sum, 1)

            def outputs_local(H, i):
                mm(bank(H, i)[0:96, :], dm[:, :], cols(fx, H, i), stop=False)
                for j in range(RT):
                    b = RT * i + j
                    mm(bank(H, i)[0:96, RC * j:RC * (j + 1)], yl[:, 0, b, :], rcols(w, H, b), start=False, stop=False)

            def outputs_carried(H, i):
                pe.wait_ge(x_ready, 4 * (H + 1))
                for j in range(RT):
                    b = RT * i + j
                    last = mm(bank(H, i)[0:96, RC * j:RC * (j + 1)], yc[:, 0, b, :], X[:, H, :, 0:NA],
                              start=False, stop=(j == RT - 1))
                last.then_inc(y_done, 1)

            def states_and_outputs(H):
                seed_sum(H)
                pe.wait_ge(ymat_ready, 2)
                outputs_local(H, 1)
                doubling(H, 0)
                outputs_local(H, 2)
                doubling(H, 1)
                outputs_local(H, 3)
                doubling(H, 2)
                doubling(H, 3)
                pe.wait_ge(x_ready, 4 * (H + 1))
                outputs_local(H, 0)
                for i in range(NT):
                    outputs_carried(H, i)

            def encode(H, i):
                k = 2 * (i % 2)
                if i < 2:
                    pe.wait_ge(fy_ready, NT * H + 2 * (i + 1))
                else:
                    pe.wait_ge(out_ready, T * H + RT * (i - 1))
                mm(bank(H, k)[0:96, :], m(M_WE), cols(fy, H, i))
                mm(bank(H, k + 1)[0:96, :], m(M_WE + 96), cols(fy, H, i)).then_inc(z_done, 1)

            def decode(H, i):
                pe.wait_ge(zz_ready, NT * H + i + 1)
                mm(bank(H, 2 * (i % 2))[0:96, :], m(M_WD), cols(zz, H, i)).then_inc(dec_done, 1)

            def h_waits(H):
                pe.wait_ge(h_act, 4 + 8 * H)
                pe.wait_ge(h_vec, 4)

            pe.wait_ge(in_early, 16)
            group_norm(0)
            h_waits(0)
            center(0, 0, h, lambda i: None)
            pe.wait_ge(in_mats, 16)
            variances(0, 0)
            group_norm(1)
            h_waits(1)
            center(0, 1, h, lambda i: None)
            variances(0, 1)
            pe.wait_ge(squared[0], 4 * NT)
            mm(bank(1, 1)[0:96, 0:1], m(M_WE), s(B2))
            mm(bank(1, 1)[0:96, 1:2], m(M_WE + 96), s(B2)).then_inc(be_done, 1)
            pe.wait_ge(bst_ready, 1)
            pe.wait_ge(rot_ready, 1)
            mm(bank(1, 2)[0:97, 0:480], bst[:, :], rotT[:, 0, 0:5, :])
            mm(bank(1, 3)[0:97, 0:288], bst[:, :], rotT[:, 0, 5:8, :]).then_inc(umat_done, 1)
            broadcast(0, 0)
            inputs(0)
            pe.wait_ge(be_ready, 1)
            broadcast(0, 1)
            inputs(1)
            states_and_outputs(0)
            states_and_outputs(1)
            for H in range(2):
                center(1, H, y2, lambda i: pe.wait_ge(y2_ready, NT * H + i + 1))
                variances(1, H)
            broadcast(1, 0)
            for H in range(2):
                for i in (0, 2):
                    encode(H, i)
                    encode(H, i + 1)
                    decode(H, i)
                    decode(H, i + 1)
                    if H == 0 and i == 0:
                        broadcast(1, 1)

        @block.vector
        def _(dve):
            n = [0]

            def chain(ins):
                n[0] += 1
                ins.then_inc(vec_chain, 1)

            def settle():
                dve.wait_ge(vec_chain, n[0])

            def stt(o, a, sca, b, op0, op1):
                return nc.vector.scalar_tensor_tensor(out=o, in0=a, scalar=sca, in1=b, op0=op0, op1=op1)

            def step_stt(*a):
                settle()
                chain(stt(*a))

            def step_ts(o, a, s1, s2, op0, op1=ALU.bypass):
                settle()
                if s2 is None:
                    chain(nc.vector.tensor_scalar(o, a, s1, None, op0))
                else:
                    chain(nc.vector.tensor_scalar(o, a, s1, s2, op0, op1))

            def step_tt(o, a, b, op):
                settle()
                chain(nc.vector.tensor_tensor(o, a, b, op))

            def expm1(p, y, arg):
                step_ts(y, arg, 1 / 128, -80 / 128, ALU.mult, ALU.max)
                step_ts(p, y, 1 / 120, None, ALU.mult)
                for c in (1 / 24, 1 / 6, 1 / 2, 1.0):
                    step_stt(p, p, c, y, ALU.add, ALU.mult)
                for _ in range(7):
                    step_stt(p, p, 2.0, p, ALU.add, ALU.mult)

            def statistics(H, q):
                dve.wait_ge(in_x[2 * H + q // 4], 16)
                nc.vector.bn_stats(st[:, HB * H + q, :], xs[:, HB * H + q, :]).then_inc(gn_stats, 1)

            def rsqrt(y, v, t, u, a):
                step_ts(a.bitcast(I32), v.bitcast(I32), 1, None, ALU.logical_shift_right)
                step_ts(y.bitcast(I32), a.bitcast(I32), -1.0, RSQRT_SEED, ALU.mult, ALU.add)
                step_stt(t, y, -0.703952253, y, ALU.mult, ALU.mult)
                step_tt(t, t, v, ALU.mult)
                step_ts(t, t, 0.703952253 * 2.38924456, None, ALU.add)
                step_tt(y, t, y, ALU.mult)
                step_tt(t, y, y, ALU.mult)
                step_tt(t, t, v, ALU.mult)
                step_ts(u, t, 0.375, -1.25, ALU.mult, ALU.add)
                step_tt(u, u, t, ALU.mult)
                step_stt(y, u, 1.875, y, ALU.add, ALU.mult)

            def group_norm(H):
                g = st[:, HB * H:HB * (H + 1), :]
                mean, de, do, q, var, scale, shift, tmp = [gn[:, H, k, 0:HB] for k in range(8)]
                dve.wait_ge(gn_mean, H + 1)
                chain(nc.vector.tensor_copy(mean, bank(H, 0)[0:96, 0:HB]))
                step_tt(de, g[:, :, 1], mean, ALU.subtract)
                chain(nc.vector.tensor_tensor(do, g[:, :, 4], mean, ALU.subtract))
                step_tt(de, de, de, ALU.mult)
                chain(nc.vector.tensor_tensor(do, do, do, ALU.mult))
                step_tt(de, de, do, ALU.add)
                chain(nc.vector.tensor_tensor(tmp, g[:, :, 2], g[:, :, 5], ALU.add))
                settle()
                stt(q, de, float(L // 2), tmp, ALU.mult, ALU.add).then_inc(gn_dev, 1)
                dve.wait_ge(gn_var, H + 1)
                chain(nc.vector.tensor_scalar(var, bank(H, 1)[0:96, 0:HB], GN_EPS, None, ALU.add))
                rsqrt(scale, var, de, do, tmp)
                settle()
                stt(shift, mean, -1.0, scale, ALU.mult, ALU.mult).then_inc(gn_scale, 1)

            def normalise(H, first, last):
                dve.wait_ge(gn_scale, H + 1)
                hv = h[:, H, :].rearrange("c (b n a) -> c n b a", b=T, n=HB)
                for k in range(first, last):
                    nc.vector.tensor_scalar(
                        hv[:, k], xs[:, HB * H + k, :].rearrange("c (a b) -> c b a", b=T),
                        gn[:, H, 5, k:k + 1], gn[:, H, 6, k:k + 1], ALU.mult, ALU.add).then_inc(h_vec, 1)

            def inverse_sigma(k, H):
                y, v, t, u, a, d = [rs[:, H, j, :] for j in range(6)]
                dve.wait_ge(variance[k], H + 1)
                chain(nc.vector.tensor_scalar(v, bank(H, 0)[0:SR, 0:CH], 1.0 / C, LN_EPS, ALU.mult, ALU.add))
                rsqrt(y, v, t, u, a)
                if k:
                    dve.wait_ge(inv_bcast[0], NT * (H + 1))
                step_ts(spl[:, H, :], y, 1.0, None, ALU.mult)
                step_tt(d, y, spl[:, H, :], ALU.subtract)
                settle()
                chain(nc.vector.tensor_copy(spl[32:64, H, :], d[32:64]))
                chain(nc.vector.tensor_copy(spl[64:SR, H, :], d[64:SR]))
                settle()
                nc.vector.tensor_tensor(spl[64:SR, H, :], d[64:SR], spl[64:SR, H, :], ALU.subtract).then_inc(inv_ready[k], 1)

            def scale_tiles(k, H, dst, gain, ready):
                for i in range(NT):
                    dve.wait_ge(inv_bcast[k], NT * H + i + 1)
                    dve.wait_ge(squared[k], 2 * (NT * H + i + 1))
                    stt(cols(dst, H, i), cols(xc, H, i), gain, bank(H, i)[0:96, :],
                        ALU.mult, ALU.mult).then_inc(ready, 1)

            def scan(H, b):
                dve.wait_ge(u_done, NT * H + b // RT + 1)
                if b == 1:
                    dve.wait_ge(w_first, H + 1)
                else:
                    dve.wait_ge(w_ready[H], b - 1)
                stt(rcols(w, H, b), rcols(w, H, b - 1), tbl(RK, 1, 1),
                    bank(H, b // RT)[0:96, RC * (b % RT):RC * (b % RT + 1)],
                    ALU.mult, ALU.add).then_inc(w_ready[H], 1)

            def doubled(H, k):
                d = 2 ** (k + 1)
                dve.wait_ge(x_sum, 5 * H + k + 2)
                o = bank(H, 0)[0:96, 0:RC].rearrange("p (n a) -> p n a", a=NA)
                xd = X[:, H, :, 1 + d:]
                nc.vector.tensor_tensor(xd, xd, o[:, :, d:], ALU.add).then_inc(x_ready, 1)

            def residual(H, i):
                dve.wait_ge(gl_ready, NT * H + i + 1)
                stt(cols(y2, H, i), cols(gl, H, i), s(B1), cols(fx, H, i), ALU.add, ALU.add).then_inc(y2_ready, 1)

            def gate(H, i):
                dve.wait_ge(gz_ready, NT * H + i + 1)
                stt(cols(zz, H, i), bank(H, 2 * (i % 2))[0:96, :], be[:, 0:1], cols(gz, H, i),
                    ALU.add, ALU.mult).then_inc(zz_ready, 1)

            def finish(H, i):
                dve.wait_ge(dec_done, NT * H + i + 1)
                dve.wait_ge(res_ready, NT * H + i + 1)
                ov = ost[:, H, :].rearrange("c (m b) -> c b m", b=T)
                stt(ov[:, RT * i:RT * (i + 1), :],
                    bank(H, 2 * (i % 2))[0:96, :].rearrange("c (b m) -> c b m", b=RT),
                    s(B2), cols(res, H, i).rearrange("c (b m) -> c b m", b=RT),
                    ALU.add, ALU.add).then_inc(out_ready, RT)

            dve.wait_ge(in_small, 16)
            expm1(scol(STEP), scol(T1), s(LS))
            step_ts(scol(STEP), scol(STEP), 1.0, None, ALU.add)
            step_tt(scol(TH), s(LI), scol(STEP), ALU.mult)
            chain(nc.vector.tensor_tensor(scol(RE), s(LR), scol(STEP), ALU.mult))
            step_ts(tbl(ANG), s(KV, NK), scol(TH), None, ALU.mult)
            step_ts(tbl(NRND), tbl(ANG), 1 / (2 * np.pi), ROUND, ALU.mult, ALU.add)
            step_ts(tbl(NRND), tbl(NRND), -ROUND, None, ALU.add)
            for part in (TWO_PI_HI, TWO_PI_MID, TWO_PI_LO):
                step_stt(tbl(ANG), tbl(NRND), -float(part), tbl(ANG), ALU.mult, ALU.add)
            settle()
            nc.vector.tensor_scalar(tbl(RED), tbl(ANG), PI_BELOW, -PI_BELOW, ALU.min, ALU.max).then_inc(angles_ready, 1)
            step_ts(tbl(XK), s(KV, NK), scol(RE), None, ALU.mult)
            for q in range(HB):
                statistics(0, q)
            expm1(tbl(EXM), tbl(TMP), tbl(XK))
            group_norm(0)
            normalise(0, HB // 2, HB)
            for q in range(HB):
                statistics(1, q)

            dve.wait_ge(sines_ready, 2)
            step_tt(tbl(AUX), tbl(SH), tbl(SH), ALU.mult)
            step_ts(tbl(AUX2), tbl(AUX), -2.0, None, ALU.mult)
            step_ts(tbl(COS), tbl(AUX2), 1.0, None, ALU.add)
            chain(nc.vector.tensor_scalar(tbl(RK), tbl(EXM), 1.0, None, ALU.add))
            chain(nc.vector.tensor_scalar(tbl(SSG), tbl(SIN), s(NRHO), None, ALU.mult))
            chain(nc.vector.tensor_scalar(tbl(NSS), tbl(SIN), s(RHO), None, ALU.mult))
            step_stt(scol(ABSI), s(LI), -1.0, s(LI), ALU.mult, ALU.max)
            step_tt(scol(ABSI), scol(ABSI), scol(STEP), ALU.mult)
            step_ts(scol(MASK), scol(ABSI), float(np.float32(2 * np.pi)) / 4, 2.0, ALU.is_lt, ALU.mult)
            step_ts(scol(MR), scol(MASK), s(NRHO), None, ALU.mult)
            chain(nc.vector.tensor_scalar(scol(MI), scol(MASK), -1.0, None, ALU.mult))
            step_tt(tbl(CM), tbl(RK), tbl(COS), ALU.mult)
            chain(nc.vector.tensor_tensor(tbl(SMG), tbl(RK), tbl(SSG), ALU.mult))
            chain(nc.vector.tensor_tensor(tbl(AUX3), tbl(RK), tbl(SIN), ALU.mult))
            chain(nc.vector.tensor_scalar(tbl(CU), tbl(COS), scol(MR), None, ALU.mult))
            chain(nc.vector.tensor_scalar(tbl(SU), tbl(SIN), scol(MI), None, ALU.mult))
            step_ts(tbl(CV, T), tbl(CM, T, 1), scol(MR), None, ALU.mult)
            chain(nc.vector.tensor_scalar(tbl(SV, T), tbl(AUX3, T, 1), scol(MI), None, ALU.mult))
            for dst, unit, mod in ((XCO, COS, CM), (XSI, SSG, SMG)):
                chain(nc.vector.tensor_copy(tbl(dst, 1), tbl(unit, 1, T - 1)))
                chain(nc.vector.tensor_tensor(tbl(dst, 1, 1), tbl(unit, 1, K15), tbl(RK, 1, T), ALU.mult))
                chain(nc.vector.tensor_copy(tbl(dst, 4, 2), tbl(mod, 4, K15 + 1)))
            step_tt(scol(T1), tbl(EXM, 1, 1), tbl(COS, 1, 1), ALU.mult)
            step_tt(scol(T1), scol(T1), tbl(AUX2, 1, 1), ALU.add)
            step_tt(scol(T2), s(LR), s(LR), ALU.mult)
            step_stt(scol(DEN), s(LI), s(LI), scol(T2), ALU.mult, ALU.add)
            step_tt(scol(T3), tbl(AUX3, 1, 1), s(LI), ALU.mult)
            settle()
            chain(nc.vector.reciprocal(scol(DEN), scol(DEN)))
            step_stt(scol(CRE), scol(T1), s(LR), scol(T3), ALU.mult, ALU.add)
            step_tt(scol(T4), scol(T1), s(LI), ALU.mult)
            step_stt(scol(CIM), tbl(AUX3, 1, 1), s(LR), scol(T4), ALU.mult, ALU.subtract)
            step_tt(scol(CRE), scol(CRE), scol(DEN), ALU.mult)
            step_tt(scol(CIM), scol(CIM), scol(DEN), ALU.mult)
            step_ts(scol(CIM), scol(CIM), s(RHO), None, ALU.mult)
            chain(nc.vector.tensor_tensor(db[:, :], s(DD), s(B1), ALU.mult))
            settle()
            dve.wait_ge(in_mats, 16)
            nc.vector.tensor_scalar(dm[:, :], m(M_ID), s(DD), None, ALU.mult).then_inc(tables_ready, 1)
            chain(nc.vector.tensor_scalar(bt1[:, :], m(M_BS), scol(CIM), None, ALU.mult))
            step_stt(bst[:, 0:C], m(M_B), scol(CRE), bt1[:, :], ALU.mult, ALU.add)
            step_tt(bt1[:, :], bst[:, 0:C], m(M_B1), ALU.mult)
            settle()
            nc.vector.reduce_sum(bst[:, C:C + 1], bt1[:, :], axis=mybir.AxisListType.X).then_inc(bst_ready, 1)

            group_norm(1)
            inverse_sigma(0, 0)
            scale_tiles(0, 0, fx, s(G1), fx_ready)
            inverse_sigma(0, 1)
            scale_tiles(0, 1, fx, s(G1), fx_ready)
            for b in range(1, T):
                scan(0, b)
            for k in range(4):
                doubled(0, k)
                scan(1, 2 * k + 1)
                if k < 3:
                    scan(1, 2 * k + 2)
            for k in range(4):
                doubled(1, k)
                residual(0, k)
            for i in range(NT):
                residual(1, i)
            dve.wait_ge(be_ready, 1)
            inverse_sigma(1, 0)
            scale_tiles(1, 0, fy, s(G2), fy_ready)
            inverse_sigma(1, 1)
            for H in range(2):
                for i in (0, 2):
                    gate(H, i)
                    gate(H, i + 1)
                    finish(H, i)
                    finish(H, i + 1)
                    if H == 0 and i == 0:
                        scale_tiles(1, 1, fy, s(G2), fy_ready)


def mode_rows(a):
    return np.concatenate([a, a])


def constants():
    eye = np.eye(96, dtype=np.float32)
    groups = np.kron(np.eye(96 // GROUP), np.ones((GROUP, GROUP))).astype(np.float32)
    swap = np.roll(eye, 48, axis=1)
    z = np.zeros((96, ZW), np.float32)
    z[:, [15, 47, 79]] = 1.0
    rho = np.repeat(np.array([-1.0, 1.0], np.float32), 48)
    mask = np.zeros((SR, NCH), np.float32)
    for k in range(SR):
        if k % 32 < NCH:
            mask[k, k % 32] = 1.0
    return (groups / np.float32(2 * GROUP), groups / np.float32(NGRP), eye - np.float32(1.0 / C), eye, swap, z,
            rho, mask)


def kernel(x, L0_conv_ln1_g, L0_conv_ln1_b, L0_conv_Lambda, L0_conv_Bmat, L0_conv_Cmat, L0_conv_D,
           L0_conv_log_step, L0_conv_ln2_g, L0_conv_ln2_b, L0_conv_W_enc, L0_conv_W_dec):
    import concourse.bacc as bacc
    from concourse.bass_utils import run_bass_kernel_spmd

    f = [np.ascontiguousarray(a) for a in (x, L0_conv_ln1_g, L0_conv_ln1_b, L0_conv_Lambda, L0_conv_Bmat,
                                           L0_conv_Cmat, L0_conv_D, L0_conv_log_step, L0_conv_ln2_g,
                                           L0_conv_ln2_b, L0_conv_W_enc, L0_conv_W_dec)]
    x, g1, b1, lam, bm, cm, dd, ls, g2, b2, we, wd = f
    mean3, var3, center, eye, swap, z, rho, mask = constants()
    powers = np.tile(np.array(POWERS, np.float32), (96, 1))
    small = np.concatenate(
        [np.stack([mode_rows(lam[:, 0]), mode_rows(lam[:, 1]), mode_rows(ls), rho, -rho, g1, b1, dd, g2, b2], 1),
         powers], 1)
    b_own = np.concatenate([bm[:, :, 0], bm[:, :, 1]])
    b_swapped = np.concatenate([bm[:, :, 1], bm[:, :, 0]])
    c_own = np.concatenate([cm[:, :, 0].T, cm[:, :, 1].T])
    c_swapped = np.concatenate([cm[:, :, 1].T, cm[:, :, 0].T])
    mats = np.concatenate([mean3, var3, center, eye, swap, b_own, b_swapped, c_own, c_swapped,
                           np.tile(b1, (96, 1)), wd.T, we.T, z], 1)
    arrays = {
        "x_dram": x.reshape(B, C, L),
        "small_dram": np.ascontiguousarray(small),
        "mats_dram": np.ascontiguousarray(mats),
        "mask_dram": mask,
    }
    nc = bacc.Bacc("TRN2", target_bir_lowering=False, num_devices=1)
    aps = {k: nc.dram_tensor(k, a.shape, mybir.dt.from_np(a.dtype), kind="ExternalInput").ap()
           for k, a in arrays.items()}
    out = nc.dram_tensor("out_dram", (B, C, L), F32, kind="ExternalOutput").ap()
    s5_block(nc, aps["x_dram"].rearrange("n c l -> c n l"), aps["small_dram"], aps["mats_dram"], aps["mask_dram"],
             out.rearrange("n c l -> c n l"))
    r = run_bass_kernel_spmd(nc, [arrays], core_ids=[0])
    return r.results[0]["out_dram"].reshape(B, C, 16, 16)
```

```python
from contextlib import ExitStack

import concourse.bass as bass
from concourse import mybir
import numpy as np

ALU = mybir.AluOpType
ACT = mybir.ActivationFunctionType
F32 = mybir.dt.float32
BF16 = mybir.dt.bfloat16
I32 = mybir.dt.int32

B, C, L = 16, 96, 256
P2 = 96
T = 8
NA = L // T
HB = B // 2
HC = HB * L
RC = HB * NA
TILE = 512
NT = HC // TILE
RT = TILE // RC
CH = 64
NCH = HC // CH
SR = 96
HV = 5
HP = 6
WARM = 4
GROUP = 3
NGRP = GROUP * L
GN_EPS = 1e-5
LN_EPS = 1e-5

POWERS = list(range(T + 1)) + [2 * T, 4 * T, 8 * T, 16 * T]
NK = len(POWERS)
K16 = POWERS.index(2 * T)
NX = 6
NDBL = 4
TWO_PI_HI = 6.28125
TWO_PI_MID = 0.0019340515136718750
TWO_PI_LO = 2 * np.pi - TWO_PI_HI - TWO_PI_MID
PI_BELOW = 3.1415925
ROUND = 1.5 * 2.0 ** 23
RSQRT_SEED = float(0x5F1FFFF9)

(LR, LI, LS, RHO, NRHO, G1, B1, DD, G2, B2, KV) = range(11)
NS = KV + NK
(M_GM, M_GV, M_P, M_ID, M_SW, M_B, M_BS, M_C, M_CS, M_B1, M_WD, M_WE) = [96 * i for i in range(12)]
M_Z = M_WE + 192
ZW = SR + NCH - 1
NM = M_Z + ZW
N_EARLY = M_ID


def s5_block(nc, x, small, mats, mask_in, out):
    ctx = ExitStack()
    with ctx:
        def sb(name, shape, dt=F32):
            return ctx.enter_context(nc.sbuf_tensor(name, shape, dt))

        def sem(name):
            return ctx.enter_context(nc.semaphore(name))

        xs = sb("xs", [C, B, L])
        h = sb("h", [C, 2, HC])
        xc = sb("xc", [C, 2, HC])
        sq = sb("sq", [C, 2, HC])
        fx = sb("fx", [C + 1, 2, HC])
        w = sb("w", [P2, 2, HC])
        y2 = sb("y2", [C, 2, HC])
        fy = sb("fy", [C, 2, HC])
        res = sb("res", [C, 2, HC])
        Z = sb("Z", [P2, 2, HB, NA])
        gl, zz, gz, ost = h, w, y2, sq

        sm = sb("sm", [96, NS])
        mt = sb("mt", [96, NM])
        rotT = sb("rotT", [96, T, 96])
        rotX = sb("rotX", [96, 2, NX, 96])
        bst = sb("bst", [96, C + 1])
        bt1 = sb("bt1", [96, C])
        um = sb("um", [C + 1, T, 96])
        yl = sb("yl", [96, 2, T, 96])
        dm = sb("dm", [96, 96])
        bcm = sb("bcm", [SR, NCH, 96], BF16)
        bcmask = sb("bcmask", [SR, NCH])
        vecs = sb("vecs", [96, 3])
        db = sb("db", [96, 1])
        tb = sb("tb", [96, 20, NK])
        sc = sb("sc", [96, 21])
        st = sb("st", [C, B, 6])
        gn = sb("gn", [C, 2, 8, HB])
        rs = sb("rs", [SR, 2, 6, CH])
        spl = sb("spl", [SR, 2, CH], BF16)

        ps = ctx.enter_context(nc.psum_tensor("ps", [128, 8, TILE], F32))

        in_small, in_early, in_mats, in_mask = sem("in_small"), sem("in_early"), sem("in_mats"), sem("in_mask")
        in_x = [sem(f"in_x{k}") for k in range(4)]
        vec_chain = sem("vec_chain")
        pool_chain = sem("pool_chain")
        angles_ready = sem("angles_ready")
        sines_ready = sem("sines_ready")
        tables_ready = sem("tables_ready")
        bst_ready = sem("bst_ready")
        rot_ready = sem("rot_ready")
        umat_done = sem("umat_done")
        um_ready = sem("um_ready")
        rotx_ready = sem("rotx_ready")
        yl_ready = sem("yl_ready")
        dm_ready = sem("dm_ready")
        bcm_ready = sem("bcm_ready")
        vecs_done = sem("vecs_done")
        vecs_ready = sem("vecs_ready")
        ones_ready = sem("ones_ready")
        gn_stats = sem("gn_stats")
        gn_mean = sem("gn_mean")
        gn_dev = sem("gn_dev")
        gn_var = sem("gn_var")
        gn_scale = sem("gn_scale")
        h_act, h_vec, h_pool = sem("h_act"), sem("h_vec"), sem("h_pool")
        centered = [sem("centered1"), sem("centered2")]
        squared = [sem("squared1"), sem("squared2")]
        variance = [sem("variance1"), sem("variance2")]
        inv_ready = [sem("inv_ready1"), sem("inv_ready2")]
        inv_bcast = [sem("inv_bcast1"), sem("inv_bcast2")]
        fx_ready, fy_ready = sem("fx_ready"), sem("fy_ready")
        u_done = sem("u_done")
        w_first = sem("w_first")
        w_local = [sem("w_local_a"), sem("w_local_b")]
        w_ready = [sem("w_ready_a"), sem("w_ready_b")]
        z_sum = sem("z_sum")
        z_seed = sem("z_seed")
        z_ready = sem("z_ready")
        y_done = sem("y_done")
        gl_ready = sem("gl_ready")
        y2_pool, y2_vec = sem("y2_pool"), sem("y2_vec")
        enc_done = sem("enc_done")
        gz_ready = sem("gz_ready")
        zz_ready = sem("zz_ready")
        dec_done = sem("dec_done")
        var_read = [sem("var_read1"), sem("var_read2")]
        res_ready = sem("res_ready")
        out_ready = sem("out_ready")
        stored = sem("stored")

        def bank(H, i):
            return ps[:, 4 * H + i, :]

        def cols(t, H, i, p=96):
            return t[0:p, H, TILE * i:TILE * (i + 1)]

        def rcols(t, H, b, p=96):
            return t[0:p, H, RC * b:RC * (b + 1)]

        def s(c, n=1):
            return sm[:, c:c + n]

        def m(c, n=96):
            return mt[:, c:c + n]

        (ANG, XK, NRND, RED, EXM, TMP, SIN, SH, SH2, CM1, COS, SSG, NSS, RK, RSIN, CU, SU, XCO, XSI,
         RSSG) = range(20)
        (STEP, Y1, TH, RE, EXP, REC, NEG, T1, T2, T3, T4, CRE, CIM, DEN, ABSI, MASK, MR, MI, EXP1, REC1, POS) = range(21)

        def tbl(k, n=NK, at=0):
            return tb[:, k, at:at + n]

        def scol(k):
            return sc[:, k:k + 1]

        Z1 = {(0, 0): (0, 0), (0, 1): (0, 2), (0, 2): (1, 1), (0, 3): (1, 3)} | {(1, i): (1, i) for i in range(NT)}
        Z2 = {(0, 0): (0, 1), (0, 1): (0, 3), (0, 2): (1, 2), (0, 3): (1, 0),
              (1, 0): (0, 0), (1, 1): (0, 2), (1, 2): (0, 1), (1, 3): (0, 3)}
        ZD = {(0, 0): (0, 0), (0, 1): (0, 2), (0, 2): (0, 1), (0, 3): (0, 3)} | {(1, i): (1, i) for i in range(NT)}

        block = ctx.enter_context(nc.Block())

        @block.sync
        def _(sp):
            for k in range(3):
                sp.dma_start(xs[:, 4 * k:4 * k + 4, :], x[:, 4 * k:4 * k + 4, :]).then_inc(in_x[k], 16)
            sp.dma_start(mt[:, N_EARLY:], mats[:, N_EARLY:]).then_inc(in_mats, 16)
            sp.dma_start(xs[:, 12:16, :], x[:, 12:16, :]).then_inc(in_x[3], 16)
            for n in range(2 * NT):
                H, i = divmod(n, NT)
                sp.wait_ge(out_ready, n + 1)
                sp.dma_start(out[:, 2 * n:2 * n + 2, :],
                             cols(ost, H, i).rearrange("c (n l) -> c n l", l=L)).then_inc(stored, 16)
            sp.wait_ge(stored, 16 * 2 * NT)

        @block.gpsimd
        def _(pool):
            n = [0]

            def chain(ins):
                n[0] += 1
                ins.then_inc(pool_chain, 1)

            def settle():
                pool.wait_ge(pool_chain, n[0])

            nc.gpsimd.memset(fx[96:97, :, :], 1.0).then_inc(ones_ready, 1)
            nc.gpsimd.memset(Z[:, :, :, 0:1], 0.0).then_inc(ones_ready, 1)
            pool.wait_ge(gn_scale, 2)
            hv = h[:, 1, :].rearrange("c (b n a) -> c n b a", b=T, n=HB)
            for k in range(HP):
                nc.gpsimd.tensor_scalar(
                    hv[:, k], xs[:, HB + k, :].rearrange("c (a b) -> c b a", b=T),
                    gn[:, 1, 5, k:k + 1], gn[:, 1, 6, k:k + 1], ALU.mult, ALU.add).then_inc(h_pool, 1)
            pool.wait_ge(in_mats, 16)

            def combine(dst, mat_a, ca, mat_b, cb, n_mats):
                def mat(c):
                    return m(c).unsqueeze(1).broadcast_to([96, n_mats, 96])

                def coef(c):
                    return c.unsqueeze(2).broadcast_to([96, n_mats, 96])

                chain(nc.gpsimd.tensor_tensor(dst[:, 0], mat(mat_a), coef(ca), ALU.mult))
                chain(nc.gpsimd.tensor_tensor(dst[:, 1], mat(mat_b), coef(cb), ALU.mult))
                settle()
                return nc.gpsimd.tensor_tensor(dst[:, 0], dst[:, 0], dst[:, 1], ALU.add)

            def second_input(H):
                yv = y2[:, H, :].rearrange("c (m b) -> c b m", b=T)
                for i in (0, 2):
                    pool.wait_ge(gl_ready, NT * H + i + 1)
                    nc.gpsimd.tensor_tensor(
                        yv[:, RT * i:RT * (i + 1), :], cols(gl, H, i).rearrange("c (b m) -> c b m", b=RT),
                        cols(fx, H, i).rearrange("c (b m) -> c b m", b=RT), ALU.add).then_inc(y2_pool, 1)

            def residual(H):
                for i in range(NT):
                    pool.wait_ge(fy_ready, NT * H + i + 1)
                    nc.gpsimd.tensor_tensor(
                        cols(res, H, i), cols(fy, H, i),
                        xs[:, HB * H + 2 * i:HB * H + 2 * i + 2, :].rearrange("c n l -> c (n l)"),
                        ALU.add).then_inc(res_ready, 1)

            pool.wait_ge(tables_ready, 1)
            combine(rotX, M_ID, tbl(XCO, NX), M_SW, tbl(XSI, NX), NX).then_inc(rotx_ready, 1)
            combine(yl, M_C, tbl(CU, T), M_CS, tbl(SU, T), T).then_inc(yl_ready, 1)
            for H in range(2):
                second_input(H)
                if H:
                    residual(0)
            residual(1)

        @block.scalar
        def _(act):
            act.dma_start(sm[:, :], small).then_inc(in_small, 16)
            act.dma_start(mt[:, 0:N_EARLY], mats[:, 0:N_EARLY]).then_inc(in_early, 16)
            act.dma_start(bcmask[:, :], mask_in).then_inc(in_mask, 16)
            act.wait_ge(angles_ready, 1)
            nc.scalar.activation(tbl(SIN), tbl(RED), ACT.Sin).then_inc(sines_ready, 1)
            nc.scalar.activation(tbl(SH), tbl(RED), ACT.Sin, scale=0.5).then_inc(sines_ready, 1)

            def normalise(H, first, last):
                act.wait_ge(gn_scale, H + 1)
                hv = h[:, H, :].rearrange("c (b n a) -> c n b a", b=T, n=HB)
                for n in range(first, last):
                    nc.scalar.activation(
                        hv[:, n], xs[:, HB * H + n, :].rearrange("c (a b) -> c b a", b=T), ACT.Identity,
                        bias=gn[:, H, 6, n:n + 1], scale=gn[:, H, 5, n:n + 1]).then_inc(h_act, 1)

            def evacuate(k, H):
                bias = vecs[:, 2:3] if k else 0.0
                if k:
                    act.wait_ge(vecs_ready, 1)
                for i in range(NT):
                    act.wait_ge(centered[k], NT * H + i + 1)
                    nc.scalar.activation(cols(sq, H, i), bank(H, i)[0:96, :], ACT.Square,
                                         bias=bias).then_inc(squared[k], 1)
                    nc.scalar.activation(cols(xc, H, i), bank(H, i)[0:96, :], ACT.Identity,
                                         bias=bias).then_inc(squared[k], 1)

            def first_state(H):
                act.wait_ge(u_done, NT * H + 1)
                nc.scalar.activation(rcols(w, H, 0), bank(H, 0)[0:96, 0:RC], ACT.Copy).then_inc(w_first, 1)

            def seed(H):
                act.wait_ge(z_sum, (1 + NDBL) * H + 1)
                nc.scalar.activation(
                    Z[:, H, :, 1:], bank(H, NT - 1)[0:96, 0:RC].rearrange("p (n a) -> p n a", a=NA)[:, :, 1:],
                    ACT.Copy).then_inc(z_seed, 1)

            def gelu_y(H):
                for i in range(NT):
                    act.wait_ge(y_done, NT * H + i + 1)
                    nc.scalar.activation(cols(gl, H, i), bank(H, i)[0:96, :], ACT.Gelu,
                                         bias=db[:, 0:1]).then_inc(gl_ready, 1)

            def gelu_z(H, i):
                act.wait_ge(enc_done, NT * H + i + 1)
                nc.scalar.activation(cols(gz, H, i), bank(*Z2[H, i])[0:96, :], ACT.Gelu,
                                     bias=vecs[:, 1:2]).then_inc(gz_ready, 1)

            act.wait_ge(in_mask, 16)
            nc.scalar.activation(bcm[:, :, :], bcmask[:, :].unsqueeze(2).broadcast_to([SR, NCH, 96]),
                                 ACT.Copy).then_inc(bcm_ready, 1)
            normalise(0, HV, HB)
            evacuate(0, 0)
            evacuate(0, 1)
            act.wait_ge(vecs_done, 1)
            nc.scalar.activation(vecs[:, :], bank(1, 1)[0:96, 0:3], ACT.Copy).then_inc(vecs_ready, 1)
            act.wait_ge(umat_done, 1)
            nc.scalar.activation(um[:, 0:5, :], bank(1, 2)[0:97, 0:480].rearrange("c (b j) -> c b j", j=96),
                                 ACT.Copy).then_inc(um_ready, 1)
            nc.scalar.activation(um[:, 5:8, :], bank(1, 3)[0:97, 0:288].rearrange("c (b j) -> c b j", j=96),
                                 ACT.Copy).then_inc(um_ready, 1)
            act.wait_ge(ones_ready, 2)
            first_state(0)
            seed(0)
            first_state(1)
            gelu_y(0)
            seed(1)
            evacuate(1, 0)
            gelu_y(1)
            evacuate(1, 1)
            for H in range(2):
                for i in range(NT):
                    gelu_z(H, i)

        @block.tensor
        def _(pe):
            def mm(o, lhsT, rhs, start=True, stop=True):
                return nc.tensor.matmul(o, lhsT, rhs, start=start, stop=stop)

            def group_mean(H):
                pe.wait_ge(gn_stats, HB * (H + 1))
                g = st[:, HB * H:HB * (H + 1), :]
                mm(bank(1, 2 * H)[0:96, 0:HB], m(M_GM), g[:, :, 1], stop=False)
                mm(bank(1, 2 * H)[0:96, 0:HB], m(M_GM), g[:, :, 4], start=False).then_inc(gn_mean, 1)

            def group_variance(H):
                pe.wait_ge(gn_dev, H + 1)
                mm(bank(1, 2 * H + 1)[0:96, 0:HB], m(M_GV), gn[:, H, 3, 0:HB]).then_inc(gn_var, 1)

            def center(k, H, src, i):
                mm(bank(H, i)[0:96, :], m(M_P), cols(src, H, i)).then_inc(centered[k], 1)

            def variances(k, H):
                for r in range(NCH):
                    if r % (TILE // CH) == 0:
                        pe.wait_ge(squared[k], 2 * (NT * H + r // (TILE // CH) + 1))
                    z = m(M_Z + NCH - 1 - r, SR)
                    last = mm(bank(H, 0)[0:SR, 0:CH], z, sq[:, H, CH * r:CH * (r + 1)],
                              start=(r == 0), stop=(r == NCH - 1))
                last.then_inc(variance[k], 1)

            def broadcast(k, H):
                pe.wait_ge(inv_ready[k], H + 1)
                for i in range(NT):
                    for j in range(TILE // CH):
                        last = mm(bank(H, i)[0:96, CH * j:CH * (j + 1)], bcm[:, TILE // CH * i + j, :], spl[:, H, :])
                    last.then_inc(inv_bcast[k], 1)

            def inputs(H, i):
                pe.wait_ge(fx_ready, NT * H + i + 1)
                for j in range(RT):
                    b = RT * i + j
                    last = mm(bank(H, i)[0:96, RC * j:RC * (j + 1)], um[:, b, :], rcols(fx, H, b, 97))
                last.then_inc(u_done, 1)

            def seed_sum(H):
                pe.wait_ge(w_local[H], T - 1)
                pe.wait_ge(rotx_ready, 1)
                w7 = rcols(w, H, T - 1).rearrange("p (n a) -> p n a", a=NA)
                o = bank(H, NT - 1)[0:96, 0:RC].rearrange("p (n a) -> p n a", a=NA)
                mm(o[:, :, 1:], rotX[:, 0, 0, :], w7[:, :, 0:NA - 1], stop=False)
                mm(o[:, :, 2:], rotX[:, 0, 1, :], w7[:, :, 0:NA - 2], start=False).then_inc(z_sum, 1)

            def doubling(H, k):
                d = 2 ** (k + 1)
                pe.wait_ge(z_seed, H + 1)
                if k:
                    pe.wait_ge(z_ready, NDBL * H + k)
                o = bank(H, NT - 1)[0:96, 0:RC].rearrange("p (n a) -> p n a", a=NA)
                mm(o[:, :, d:], rotX[:, 0, 2 + k, :], Z[:, H, :, 0:NA - d]).then_inc(z_sum, 1)

            def direct(H, i):
                if i < NT - 1:
                    pe.wait_ge(w_local[H], RT * (i + 1) - 1)
                else:
                    pe.wait_ge(z_ready, NDBL * (H + 1))
                mm(bank(H, i)[0:96, :], dm[:, :], cols(fx, H, i), stop=False)

            def outputs(H, i):
                for j in range(RT):
                    b = RT * i + j
                    pe.wait_ge(w_ready[H], b + 1)
                    last = mm(bank(H, i)[0:96, RC * j:RC * (j + 1)], yl[:, 0, b, :], rcols(w, H, b),
                              start=False, stop=(j == RT - 1))
                last.then_inc(y_done, 1)

            def encode(H, i):
                if H == 0:
                    pe.wait_ge(fy_ready, (2, 4, 4, 4)[i])
                    if i == 2:
                        pe.wait_ge(squared[1], 2 * (NT + 3))
                    if i == 3:
                        pe.wait_ge(squared[1], 4 * NT)
                        pe.wait_ge(var_read[1], 2)
                else:
                    pe.wait_ge(fy_ready, NT + i + 1)
                    pe.wait_ge(out_ready, (1, 2, 3, 4)[i])
                mm(bank(*Z1[H, i])[0:96, :], m(M_WE), cols(fy, H, i))
                mm(bank(*Z2[H, i])[0:96, :], m(M_WE + 96), cols(fy, H, i)).then_inc(enc_done, 1)

            def decode(H, i):
                pe.wait_ge(zz_ready, NT * H + i + 1)
                mm(bank(*ZD[H, i])[0:96, :], m(M_WD), cols(zz, H, i)).then_inc(dec_done, 1)

            pe.wait_ge(in_early, 16)
            group_mean(0)
            group_variance(0)
            for _ in range(WARM):
                mm(bank(0, 0)[0:96, 0:192], m(M_P), mt[:, 0:192])
            group_mean(1)
            pe.wait_ge(h_vec, HV)
            pe.wait_ge(h_act, HB - HV)
            center(0, 0, h, 0)
            center(0, 0, h, 1)
            group_variance(1)
            center(0, 0, h, 2)
            center(0, 0, h, 3)
            pe.wait_ge(in_mats, 16)
            variances(0, 0)
            pe.wait_ge(h_pool, HP)
            pe.wait_ge(h_vec, HV + HB - HP)
            for i in range(NT):
                center(0, 1, h, i)
            pe.wait_ge(squared[0], 2 * (NT + 2))
            mm(bank(1, 1)[0:96, 0:1], m(M_WE), s(B2))
            mm(bank(1, 1)[0:96, 1:2], m(M_WE + 96), s(B2))
            mm(bank(1, 1)[0:96, 2:3], m(M_P), s(B1)).then_inc(vecs_done, 1)
            variances(0, 1)
            pe.wait_ge(bst_ready, 1)
            pe.wait_ge(rot_ready, 1)
            mm(bank(1, 2)[0:97, 0:480], bst[:, :], rotT[:, 0:5, :])
            mm(bank(1, 3)[0:97, 0:288], bst[:, :], rotT[:, 5:8, :]).then_inc(umat_done, 1)
            pe.wait_ge(bcm_ready, 1)
            broadcast(0, 0)
            pe.wait_ge(um_ready, 2)
            pe.wait_ge(ones_ready, 1)
            for i in range(NT):
                inputs(0, i)
            pe.wait_ge(dm_ready, 1)
            for i in range(NT - 1):
                direct(0, i)
            pe.wait_ge(vecs_ready, 1)
            broadcast(0, 1)
            seed_sum(0)
            for i in range(NT):
                inputs(1, i)
                doubling(0, i)
            direct(0, NT - 1)
            pe.wait_ge(yl_ready, 1)
            for i in range(NT - 1):
                outputs(0, i)
                direct(1, i)
            outputs(0, NT - 1)
            seed_sum(1)
            pe.wait_ge(y2_pool, 2)
            pe.wait_ge(y2_vec, 2)
            for i in range(NT):
                center(1, 0, y2, i)
                doubling(1, i)
            variances(1, 0)
            direct(1, NT - 1)
            for i in range(NT):
                outputs(1, i)
            broadcast(1, 0)
            pe.wait_ge(y2_pool, 4)
            pe.wait_ge(y2_vec, 4)
            for i in range(NT):
                center(1, 1, y2, i)
            variances(1, 1)
            for i in range(NT):
                encode(0, i)
            for i in range(NT):
                decode(0, i)
            broadcast(1, 1)
            encode(1, 0)
            encode(1, 1)
            decode(1, 0)
            encode(1, 2)
            decode(1, 1)
            encode(1, 3)
            decode(1, 2)
            decode(1, 3)

        @block.vector
        def _(dve):
            n = [0]

            def chain(ins):
                n[0] += 1
                ins.then_inc(vec_chain, 1)

            def settle():
                dve.wait_ge(vec_chain, n[0])

            def stt(o, a, sca, b, op0, op1):
                return nc.vector.scalar_tensor_tensor(out=o, in0=a, scalar=sca, in1=b, op0=op0, op1=op1)

            def step_stt(*a):
                settle()
                chain(stt(*a))

            def step_ts(o, a, s1, s2, op0, op1=None):
                settle()
                if s2 is None:
                    chain(nc.vector.tensor_scalar(o, a, s1, None, op0))
                else:
                    chain(nc.vector.tensor_scalar(o, a, s1, s2, op0, op1))

            def step_tt(o, a, b, op):
                settle()
                chain(nc.vector.tensor_tensor(o, a, b, op))

            def expm1(p, y, arg, between=lambda j: None):
                step_ts(y, arg, 1 / 128, -80 / 128, ALU.mult, ALU.max)
                between(0)
                step_ts(p, y, 1 / 120, None, ALU.mult)
                between(1)
                for j, c in enumerate((1 / 24, 1 / 6, 1 / 2, 1.0)):
                    step_stt(p, p, c, y, ALU.add, ALU.mult)
                    between(2 + j)
                for j in range(7):
                    step_stt(p, p, 2.0, p, ALU.add, ALU.mult)
                    between(6 + j)

            def statistics(H, q):
                if q % 4 == 0:
                    dve.wait_ge(in_x[2 * H + q // 4], 16)
                nc.vector.bn_stats(st[:, HB * H + q, :], xs[:, HB * H + q, :]).then_inc(gn_stats, 1)

            def rsqrt(y, v, t, u, a, between=lambda j: None):
                step_ts(a.bitcast(I32), v.bitcast(I32), 1, None, ALU.logical_shift_right)
                between(0)
                step_ts(y.bitcast(I32), a.bitcast(I32), -1.0, RSQRT_SEED, ALU.mult, ALU.add)
                between(1)
                step_stt(t, y, -0.703952253, y, ALU.mult, ALU.mult)
                between(2)
                step_tt(t, t, v, ALU.mult)
                between(3)
                step_stt(y, t, 0.703952253 * 2.38924456, y, ALU.add, ALU.mult)
                between(4)
                step_tt(t, y, y, ALU.mult)
                between(5)
                step_tt(t, t, v, ALU.mult)
                between(6)
                step_ts(u, t, 0.375, -1.25, ALU.mult, ALU.add)
                between(7)
                step_tt(u, u, t, ALU.mult)
                between(8)
                step_stt(y, u, 1.875, y, ALU.add, ALU.mult)

            def group_norm(H, between=lambda j: None, between_parts=lambda: None):
                g = st[:, HB * H:HB * (H + 1), :]
                mean, de, do, q, var, scale, shift, tmp = [gn[:, H, k, 0:HB] for k in range(8)]
                dve.wait_ge(gn_mean, H + 1)
                chain(nc.vector.tensor_copy(mean, bank(1, 2 * H)[0:96, 0:HB]))
                step_tt(de, g[:, :, 1], mean, ALU.subtract)
                chain(nc.vector.tensor_tensor(do, g[:, :, 4], mean, ALU.subtract))
                chain(nc.vector.tensor_tensor(tmp, g[:, :, 2], g[:, :, 5], ALU.add))
                step_tt(de, de, de, ALU.mult)
                chain(nc.vector.tensor_tensor(do, do, do, ALU.mult))
                step_tt(de, de, do, ALU.add)
                settle()
                stt(q, de, float(L // 2), tmp, ALU.mult, ALU.add).then_inc(gn_dev, 1)
                between_parts()
                dve.wait_ge(gn_var, H + 1)
                chain(nc.vector.tensor_scalar(var, bank(1, 2 * H + 1)[0:96, 0:HB], GN_EPS, None, ALU.add))
                rsqrt(scale, var, de, do, tmp, between)
                settle()
                stt(shift, mean, -1.0, scale, ALU.mult, ALU.mult).then_inc(gn_scale, 1)

            def normalise(H, first, last):
                dve.wait_ge(gn_scale, H + 1)
                hv = h[:, H, :].rearrange("c (b n a) -> c n b a", b=T, n=HB)
                for k in range(first, last):
                    nc.vector.tensor_scalar(
                        hv[:, k], xs[:, HB * H + k, :].rearrange("c (a b) -> c b a", b=T),
                        gn[:, H, 5, k:k + 1], gn[:, H, 6, k:k + 1], ALU.mult, ALU.add).then_inc(h_vec, 1)

            def inverse_sigma(k, H, between=lambda j: None):
                y, v, t, u, a, d = [rs[:, H, j, :] for j in range(6)]
                dve.wait_ge(variance[k], H + 1)
                nc.vector.tensor_scalar(v, bank(H, 0)[0:SR, 0:CH], 1.0 / C, LN_EPS,
                                        ALU.mult, ALU.add).then_inc(var_read[k], 1)
                dve.wait_ge(var_read[k], H + 1)
                between(-1)
                rsqrt(y, v, t, u, a, between)
                between(9)
                if k:
                    dve.wait_ge(inv_bcast[0], NT * (H + 1))
                step_ts(spl[:, H, :], y, 1.0, None, ALU.mult)
                between(10)
                step_tt(d, y, spl[:, H, :], ALU.subtract)
                between(11)
                settle()
                chain(nc.vector.tensor_copy(spl[32:64, H, :], d[32:64]))
                chain(nc.vector.tensor_copy(spl[64:SR, H, :], d[64:SR]))
                between(12)
                settle()
                nc.vector.tensor_tensor(spl[64:SR, H, :], d[64:SR], spl[64:SR, H, :], ALU.subtract).then_inc(inv_ready[k], 1)

            def scale_tile(k, H, i, dst, gain, ready):
                dve.wait_ge(inv_bcast[k], NT * H + i + 1)
                stt(cols(dst, H, i), cols(xc, H, i), gain, bank(H, i)[0:96, :],
                    ALU.mult, ALU.mult).then_inc(ready, 1)

            def scan(H, b):
                dve.wait_ge(u_done, NT * H + b // RT + 1)
                if b == 1:
                    dve.wait_ge(w_first, H + 1)
                else:
                    dve.wait_ge(w_local[H], b - 1)
                stt(rcols(w, H, b), rcols(w, H, b - 1), tbl(RK, 1, 1),
                    bank(H, b // RT)[0:96, RC * (b % RT):RC * (b % RT + 1)],
                    ALU.mult, ALU.add).then_inc(w_local[H], 1)

            def doubled(H, k):
                d = 2 ** (k + 1)
                dve.wait_ge(z_sum, (1 + NDBL) * H + k + 2)
                o = bank(H, NT - 1)[0:96, 0:RC].rearrange("p (n a) -> p n a", a=NA)
                zd = Z[:, H, :, d:]
                nc.vector.tensor_tensor(zd, zd, o[:, :, d:], ALU.add).then_inc(z_ready, 1)

            def carry(H, b):
                dve.wait_ge(z_ready, NDBL * (H + 1))
                stt(rcols(w, H, b), Z[:, H].rearrange("p n a -> p (n a)"), tbl(RK, 1, b), rcols(w, H, b),
                    ALU.mult, ALU.add).then_inc(w_ready[H], 1)

            def gate(H, i):
                dve.wait_ge(gz_ready, NT * H + i + 1)
                stt(cols(zz, H, i), bank(*Z1[H, i])[0:96, :], vecs[:, 0:1], cols(gz, H, i),
                    ALU.add, ALU.mult).then_inc(zz_ready, 1)

            def finish(H, i):
                dve.wait_ge(dec_done, NT * H + i + 1)
                dve.wait_ge(res_ready, NT * H + i + 1)
                stt(cols(ost, H, i), bank(*ZD[H, i])[0:96, :], s(B2), cols(res, H, i),
                    ALU.add, ALU.add).then_inc(out_ready, 1)

            dve.wait_ge(in_small, 16)
            step_stt(scol(REC), s(LS), -1.0, s(LS), ALU.mult, ALU.max)
            expm1(scol(EXP), scol(Y1), scol(REC), lambda j: statistics(0, j - 5) if j >= 5 else None)
            step_ts(scol(EXP1), scol(EXP), 1.0, None, ALU.add)
            chain(nc.vector.tensor_scalar(scol(NEG), s(LS), 0.0, None, ALU.is_lt))
            chain(nc.vector.tensor_scalar(scol(POS), s(LS), 0.0, None, ALU.is_ge))
            settle()
            chain(nc.vector.reciprocal(scol(REC1), scol(EXP1)))
            step_tt(scol(T4), scol(REC1), scol(NEG), ALU.mult)
            step_stt(scol(STEP), scol(EXP1), scol(POS), scol(T4), ALU.mult, ALU.add)
            step_tt(scol(TH), s(LI), scol(STEP), ALU.mult)
            chain(nc.vector.tensor_tensor(scol(RE), s(LR), scol(STEP), ALU.mult))
            step_ts(tbl(ANG), s(KV, NK), scol(TH), None, ALU.mult)
            step_ts(tbl(NRND), tbl(ANG), 1 / (2 * np.pi), ROUND, ALU.mult, ALU.add)
            step_ts(tbl(NRND), tbl(NRND), -ROUND, None, ALU.add)
            for part in (TWO_PI_HI, TWO_PI_MID, TWO_PI_LO):
                step_stt(tbl(ANG), tbl(NRND), -float(part), tbl(ANG), ALU.mult, ALU.add)
            settle()
            nc.vector.tensor_scalar(tbl(RED), tbl(ANG), PI_BELOW, -PI_BELOW, ALU.min, ALU.max).then_inc(angles_ready, 1)
            group_norm(0, lambda j: statistics(1, j) if j < 8 else None)
            normalise(0, 0, HV)
            group_norm(1)
            normalise(1, HP, HB)
            step_ts(tbl(XK), s(KV, NK), scol(RE), None, ALU.mult)
            expm1(tbl(EXM), tbl(TMP), tbl(XK))

            dve.wait_ge(sines_ready, 2)
            step_tt(tbl(SH2), tbl(SH), tbl(SH), ALU.mult)
            chain(nc.vector.tensor_scalar(tbl(NSS), tbl(SIN), s(RHO), None, ALU.mult))
            chain(nc.vector.tensor_scalar(tbl(RK), tbl(EXM), 1.0, None, ALU.add))
            step_ts(tbl(CM1), tbl(SH2), -2.0, None, ALU.mult)
            step_tt(tbl(RSIN), tbl(RK), tbl(SIN), ALU.mult)
            step_ts(tbl(COS), tbl(CM1), 1.0, None, ALU.add)
            step_tt(scol(T1), tbl(EXM, 1, 1), tbl(COS, 1, 1), ALU.mult)
            dve.wait_ge(in_mats, 16)
            for b in range(T):
                chain(nc.vector.tensor_scalar(rotT[:, b, :], m(M_ID), tbl(COS, 1, b), None, ALU.mult))
            chain(nc.vector.tensor_tensor(scol(T2), s(LR), s(LR), ALU.mult))
            step_tt(scol(T1), scol(T1), tbl(CM1, 1, 1), ALU.add)
            chain(stt(scol(DEN), s(LI), s(LI), scol(T2), ALU.mult, ALU.add))
            chain(nc.vector.tensor_tensor(scol(T3), tbl(RSIN, 1, 1), s(LI), ALU.mult))
            settle()
            for b in range(T):
                last = stt(rotT[:, b, :], m(M_SW), tbl(NSS, 1, b), rotT[:, b, :], ALU.mult, ALU.add)
                if b < T - 1:
                    chain(last)
            last.then_inc(rot_ready, 1)
            chain(nc.vector.reciprocal(scol(DEN), scol(DEN)))
            chain(nc.vector.tensor_tensor(scol(T4), scol(T1), s(LI), ALU.mult))
            step_stt(scol(CRE), scol(T1), s(LR), scol(T3), ALU.mult, ALU.add)
            chain(stt(scol(CIM), tbl(RSIN, 1, 1), s(LR), scol(T4), ALU.mult, ALU.subtract))
            step_tt(scol(CRE), scol(CRE), scol(DEN), ALU.mult)
            step_stt(scol(CIM), scol(CIM), scol(DEN), s(RHO), ALU.mult, ALU.mult)
            step_ts(bt1[:, :], m(M_BS), scol(CIM), None, ALU.mult)
            step_stt(bst[:, 0:C], m(M_B), scol(CRE), bt1[:, :], ALU.mult, ALU.add)
            step_tt(bt1[:, :], bst[:, 0:C], m(M_B1), ALU.mult)
            settle()
            nc.vector.reduce_sum(bst[:, C:C + 1], bt1[:, :], axis=mybir.AxisListType.X).then_inc(bst_ready, 1)

            def output_tables():
                chain(stt(scol(ABSI), s(LI), -1.0, s(LI), ALU.mult, ALU.max))
                chain(nc.vector.tensor_scalar(tbl(SSG), tbl(SIN), s(NRHO), None, ALU.mult))
                step_tt(scol(ABSI), scol(ABSI), scol(STEP), ALU.mult)
                chain(nc.vector.tensor_tensor(tbl(RSSG), tbl(RK), tbl(SSG), ALU.mult))
                step_ts(scol(MASK), scol(ABSI), float(np.float32(2 * np.pi)) / 4, 2.0, ALU.is_lt, ALU.mult)
                step_ts(scol(MR), scol(MASK), s(NRHO), None, ALU.mult)
                chain(nc.vector.tensor_scalar(scol(MI), scol(MASK), -1.0, None, ALU.mult))
                step_ts(tbl(CU), tbl(COS), scol(MR), None, ALU.mult)
                chain(nc.vector.tensor_scalar(tbl(SU), tbl(SIN), scol(MI), None, ALU.mult))
                for dst, unit in ((XCO, COS), (XSI, SSG)):
                    chain(stt(tbl(dst, 1, 0), tbl(unit, 1, T), tbl(RK, 1, 1), tbl(RK, 1, 0),
                              ALU.mult, ALU.mult))
                    chain(stt(tbl(dst, 1, 1), tbl(unit, 1, K16), tbl(RK, 1, 1), tbl(RK, 1, T), ALU.mult, ALU.mult))
                    chain(nc.vector.tensor_tensor(tbl(dst, 4, 2), tbl(unit, 4, K16), tbl(RK, 4, K16), ALU.mult))
                settle()
                nc.vector.tensor_tensor(db[:, :], s(DD), s(B1), ALU.mult).then_inc(tables_ready, 1)
                nc.vector.tensor_scalar(dm[:, :], m(M_ID), s(DD), None, ALU.mult).then_inc(dm_ready, 1)

            def second_input(H, i):
                dve.wait_ge(gl_ready, NT * H + i + 1)
                yv = y2[:, H, :].rearrange("c (m b) -> c b m", b=T)
                nc.vector.tensor_tensor(
                    yv[:, RT * i:RT * (i + 1), :], cols(gl, H, i).rearrange("c (b m) -> c b m", b=RT),
                    cols(fx, H, i).rearrange("c (b m) -> c b m", b=RT), ALU.add).then_inc(y2_vec, 1)

            inverse_sigma(0, 0)
            output_tables()
            for i in range(NT):
                scale_tile(0, 0, i, fx, s(G1), fx_ready)
            inverse_sigma(0, 1, lambda j: scan(0, j // 2 + 1) if j >= 0 and j % 2 == 0 else None)
            scale_tile(0, 1, 0, fx, s(G1), fx_ready)
            for i in range(NT):
                if i < NT - 1:
                    scale_tile(0, 1, i + 1, fx, s(G1), fx_ready)
                doubled(0, i)
            for b in range(T):
                carry(0, b)
                if b < T - 1:
                    scan(1, b + 1)
            second_input(0, 1)
            second_input(0, 3)
            for k in range(NDBL):
                doubled(1, k)
            for b in range(T):
                carry(1, b)
            inverse_sigma(1, 0, lambda j: second_input(1, 1 if j < 8 else 3) if j in (6, 11) else None)
            for i in range(NT):
                scale_tile(1, 0, i, fy, s(G2), fy_ready)
            dve.wait_ge(vecs_ready, 1)
            inverse_sigma(1, 1, lambda j: gate(0, j // 4 - 1) if j in (4, 8, 12) else None)
            gate(0, 3)
            finish(0, 0)
            finish(0, 1)
            scale_tile(1, 1, 0, fy, s(G2), fy_ready)
            finish(0, 2)
            scale_tile(1, 1, 1, fy, s(G2), fy_ready)
            finish(0, 3)
            scale_tile(1, 1, 2, fy, s(G2), fy_ready)
            scale_tile(1, 1, 3, fy, s(G2), fy_ready)
            gate(1, 0)
            gate(1, 1)
            finish(1, 0)
            gate(1, 2)
            finish(1, 1)
            gate(1, 3)
            finish(1, 2)
            finish(1, 3)


def mode_rows(a):
    return np.concatenate([a, a])


def constants():
    eye = np.eye(96, dtype=np.float32)
    groups = np.kron(np.eye(96 // GROUP), np.ones((GROUP, GROUP))).astype(np.float32)
    swap = np.roll(eye, 48, axis=1)
    z = np.zeros((96, ZW), np.float32)
    z[:, NCH - 1::NCH] = 1.0
    rho = np.repeat(np.array([-1.0, 1.0], np.float32), 48)
    mask = np.zeros((SR, NCH), np.float32)
    mask[np.arange(SR), np.arange(SR) % NCH] = 1.0
    return (groups / np.float32(2 * GROUP), groups / np.float32(NGRP), eye - np.float32(1.0 / C), eye, swap, z,
            rho, mask)


def kernel(x, L0_conv_ln1_g, L0_conv_ln1_b, L0_conv_Lambda, L0_conv_Bmat, L0_conv_Cmat, L0_conv_D,
           L0_conv_log_step, L0_conv_ln2_g, L0_conv_ln2_b, L0_conv_W_enc, L0_conv_W_dec):
    import concourse.bacc as bacc
    from concourse.bass_utils import run_bass_kernel_spmd

    f = [np.ascontiguousarray(a) for a in (x, L0_conv_ln1_g, L0_conv_ln1_b, L0_conv_Lambda, L0_conv_Bmat,
                                           L0_conv_Cmat, L0_conv_D, L0_conv_log_step, L0_conv_ln2_g,
                                           L0_conv_ln2_b, L0_conv_W_enc, L0_conv_W_dec)]
    x, g1, b1, lam, bm, cm, dd, ls, g2, b2, we, wd = f
    mean3, var3, center, eye, swap, z, rho, mask = constants()
    powers = np.tile(np.array(POWERS, np.float32), (96, 1))
    small = np.concatenate(
        [np.stack([mode_rows(lam[:, 0]), mode_rows(lam[:, 1]), mode_rows(ls), rho, -rho, g1, b1, dd, g2, b2], 1),
         powers], 1)
    b_own = np.concatenate([bm[:, :, 0], bm[:, :, 1]])
    b_swapped = np.concatenate([bm[:, :, 1], bm[:, :, 0]])
    c_own = np.concatenate([cm[:, :, 0].T, cm[:, :, 1].T])
    c_swapped = np.concatenate([cm[:, :, 1].T, cm[:, :, 0].T])
    mats = np.concatenate([mean3, var3, center, eye, swap, b_own, b_swapped, c_own, c_swapped,
                           np.tile(b1, (96, 1)), wd.T, we.T, z], 1)
    arrays = {
        "x_dram": x.reshape(B, C, L),
        "small_dram": np.ascontiguousarray(small),
        "mats_dram": np.ascontiguousarray(mats),
        "mask_dram": mask,
    }
    nc = bacc.Bacc("TRN2", target_bir_lowering=False, num_devices=1)
    aps = {k: nc.dram_tensor(k, a.shape, mybir.dt.from_np(a.dtype), kind="ExternalInput").ap()
           for k, a in arrays.items()}
    out = nc.dram_tensor("out_dram", (B, C, L), F32, kind="ExternalOutput").ap()
    s5_block(nc, aps["x_dram"].rearrange("n c l -> c n l"), aps["small_dram"], aps["mats_dram"], aps["mask_dram"],
             out.rearrange("n c l -> c n l"))
    r = run_bass_kernel_spmd(nc, [arrays], core_ids=[0])
    return r.results[0]["out_dram"].reshape(B, C, 16, 16)
```

```python
from contextlib import ExitStack

import concourse.bass as bass
from concourse import mybir
import numpy as np

ALU = mybir.AluOpType
ACT = mybir.ActivationFunctionType
F32 = mybir.dt.float32
BF16 = mybir.dt.bfloat16
I32 = mybir.dt.int32

B, C, L = 16, 96, 256
P2 = 96
T = 8
NA = L // T
HB = B // 2
HC = HB * L
RC = HB * NA
TILE = 512
NT = HC // TILE
RT = TILE // RC
CH = 64
NCH = HC // CH
NPART = 3
SR = NPART * NCH
LOADS = ((0, 2), (2, 4), (4, 8), (8, 12), (12, 16))
WARM = (7, 2, 10)
FIRST_PM = 4
GROUP = 3
NGRP = GROUP * L
GN_EPS = 1e-5
LN_EPS = 1e-5

POWERS = list(range(T + 1)) + [2 * T, 4 * T, 8 * T, 16 * T]
NK = len(POWERS)
K16 = POWERS.index(2 * T)
NX = 6
NDBL = 4
TWO_PI_HI = 6.28125
TWO_PI_MID = 0.0019340515136718750
TWO_PI_LO = 2 * np.pi - TWO_PI_HI - TWO_PI_MID
PI_BELOW = 3.1415925
ROUND = 1.5 * 2.0 ** 23
RSQRT_SEED = float(0x5F1FFFF9)
RSQRT_SCALE = 64.0 / 9.0

(LR, LI, LS, RHO, NRHO, G1, B1, DD, G2, B2, KV) = range(11)
NS = KV + NK
(M_NM, M_GD, M_GV, M_P, M_ID, M_SW, M_B, M_BS, M_C, M_CS, M_B1, M_WD, M_WE) = [96 * i for i in range(13)]
M_Z = M_WE + 192
ZW = 2 * NCH - 1
NM = M_Z + ZW
N_EARLY = M_SW


def s5_block(nc, x, small, mats, mask_in, out):
    ctx = ExitStack()
    with ctx:
        def sb(name, shape, dt=F32):
            return ctx.enter_context(nc.sbuf_tensor(name, shape, dt))

        def sem(name):
            return ctx.enter_context(nc.semaphore(name))

        xs = sb("xs", [C, B, L])
        gl = sb("gl", [C, 2, HC])
        xc = sb("xc", [C, 2, HC])
        sq = sb("sq", [C, 2, HC])
        fx = sb("fx", [C + 1, 2, HC])
        w = sb("w", [P2, 2, HC])
        y2 = sb("y2", [C, 2, HC])
        fy = sb("fy", [C, 2, HC])
        res = sb("res", [C, 2, HC])
        Z = sb("Z", [P2, 2, HB, NA])
        zz, gz, ost = w, y2, sq

        sm = sb("sm", [96, NS])
        mt = sb("mt", [96, NM])
        rotT = sb("rotT", [96, T, 96])
        rotX = sb("rotX", [96, 2, NX, 96])
        bst = sb("bst", [96, C + 1])
        bt1 = sb("bt1", [96, C])
        um = sb("um", [C + 1, T, 96])
        yl = sb("yl", [96, 2, T, 96])
        dm = sb("dm", [96, 96])
        pm = sb("pm", [96, B, 96])
        bcm = sb("bcm", [SR, NCH, 96], BF16)
        cmask = sb("cmask", [SR, NCH])
        vecs = sb("vecs", [96, 3])
        db = sb("db", [96, 1])
        tb = sb("tb", [96, 20, NK])
        sc = sb("sc", [96, 21])
        st = sb("st", [C, B, 6])
        gn = sb("gn", [C, 2, 7, HB])
        (G_VAR, G_T, G_U, G_MINUS, G_SCALE, G_SHIFT, G_BIAS) = range(7)
        gdev = sb("gdev", [C, 2, HB, 2])
        rs = sb("rs", [NCH, 2, 4, CH])
        midc = sb("midc", [NCH, 2, CH], BF16)
        parts = sb("parts", [SR, 2, CH], BF16)

        ps = ctx.enter_context(nc.psum_tensor("ps", [128, 8, TILE], F32))

        in_small, in_early, in_mats, in_mask = sem("in_small"), sem("in_early"), sem("in_mats"), sem("in_mask")
        in_x = [sem(f"in_x{k}") for k in range(len(LOADS))]
        norm_steps = sem("norm_steps")
        par_steps = sem("par_steps")
        pool_chain = sem("pool_chain")
        angles_ready = sem("angles_ready")
        sines_ready = sem("sines_ready")
        cos_ready = sem("cos_ready")
        rotcos_ready = sem("rotcos_ready")
        rot_ready = sem("rot_ready")
        bst_ready = sem("bst_ready")
        umat_done = sem("umat_done")
        um_ready = sem("um_ready")
        tables_ready = sem("tables_ready")
        rotx_ready = sem("rotx_ready")
        yl_ready = sem("yl_ready")
        dm_ready = sem("dm_ready")
        bcm_ready = sem("bcm_ready")
        vecs_done = sem("vecs_done")
        vecs_ready = sem("vecs_ready")
        ones_ready = sem("ones_ready")
        gn_stats = sem("gn_stats")
        gn_mean = sem("gn_mean")
        gn_dev = sem("gn_dev")
        gn_var = sem("gn_var")
        gn_shift = sem("gn_shift")
        bias_done = sem("bias_done")
        bias_ready = sem("bias_ready")
        pm_ready = sem("pm_ready")
        centered = [sem("centered1"), sem("centered2")]
        squared = [sem("squared1"), sem("squared2")]
        taken = [sem("taken1"), sem("taken2")]
        variance = [sem("variance1"), sem("variance2")]
        var_read = sem("var_read")
        inv_ready = [sem("inv_ready1"), sem("inv_ready2")]
        inv_bcast = [sem("inv_bcast1"), sem("inv_bcast2")]
        fx_ready = sem("fx_ready")
        fy_ready = sem("fy_ready")
        u_done = sem("u_done")
        w_first = sem("w_first")
        w_local = [sem("w_local_a"), sem("w_local_b")]
        w_ready = [sem("w_ready_a"), sem("w_ready_b")]
        z_sum = sem("z_sum")
        z_seed = sem("z_seed")
        z_ready = sem("z_ready")
        y_done = sem("y_done")
        gl_ready = sem("gl_ready")
        y2_pool = sem("y2_pool")
        y2_vec = sem("y2_vec")
        enc_done = sem("enc_done")
        gz_ready = sem("gz_ready")
        zz_ready = sem("zz_ready")
        dec_done = sem("dec_done")
        res_ready = sem("res_ready")
        out_ready = sem("out_ready")
        stored = sem("stored")

        def bank(H, i):
            return ps[:, 4 * H + i, :]

        def cols(t, H, i, p=96):
            return t[0:p, H, TILE * i:TILE * (i + 1)]

        def rcols(t, H, b, p=96):
            return t[0:p, H, RC * b:RC * (b + 1)]

        def s(c, n=1):
            return sm[:, c:c + n]

        def m(c, n=96):
            return mt[:, c:c + n]

        (ANG, XK, NRND, RED, EXM, TMP, SIN, SH, SH2, CM1, COS, SSG, NSS, RK, RSIN, CU, SU, XCO, XSI,
         RSSG) = range(20)
        (STEP, Y1, TH, RE, EXP, REC, NEG, T1, T2, T3, T4, CRE, CIM, DEN, ABSI, MASK, MR, MI, EXP1, REC1, POS) = range(21)

        def tbl(k, n=NK, at=0):
            return tb[:, k, at:at + n]

        def scol(k):
            return sc[:, k:k + 1]

        Z1 = {(0, 0): (0, 0), (0, 1): (0, 2), (0, 2): (1, 1), (0, 3): (1, 3)} | {(1, i): (1, i) for i in range(NT)}
        Z2 = {(0, 0): (0, 1), (0, 1): (0, 3), (0, 2): (1, 2), (0, 3): (1, 0),
              (1, 0): (0, 0), (1, 1): (0, 2), (1, 2): (0, 1), (1, 3): (0, 3)}
        ZD = {(0, 0): (0, 0), (0, 1): (0, 2), (0, 2): (0, 1), (0, 3): (0, 3)} | {(1, i): (1, i) for i in range(NT)}

        block = ctx.enter_context(nc.Block())

        @block.sync
        def _(sp):
            for k, (first, last) in enumerate(LOADS):
                if last == B:
                    sp.dma_start(mt[:, N_EARLY:], mats[:, N_EARLY:]).then_inc(in_mats, 16)
                sp.dma_start(xs[:, first:last, :], x[:, first:last, :]).then_inc(in_x[k], 16)
            for n in range(2 * NT):
                H, i = divmod(n, NT)
                sp.wait_ge(out_ready, n + 1)
                sp.dma_start(out[:, 2 * n:2 * n + 2, :],
                             cols(ost, H, i).rearrange("c (n l) -> c n l", l=L)).then_inc(stored, 16)
            sp.wait_ge(stored, 16 * 2 * NT)

        @block.gpsimd
        def _(pool):
            n = [0]

            def chain(ins):
                n[0] += 1
                ins.then_inc(pool_chain, 1)

            def settle():
                pool.wait_ge(pool_chain, n[0])

            nc.gpsimd.memset(fx[96:97, :, :], 1.0).then_inc(ones_ready, 1)
            nc.gpsimd.memset(Z[:, :, :, 0:1], 0.0).then_inc(ones_ready, 1)
            pool.wait_ge(cos_ready, 1)
            nc.gpsimd.tensor_tensor(
                rotT[:, :, :], m(M_ID).unsqueeze(1).broadcast_to([96, T, 96]),
                tbl(COS, T).unsqueeze(2).broadcast_to([96, T, 96]), ALU.mult).then_inc(rotcos_ready, 1)
            pool.wait_ge(in_mats, 16)

            def combine(dst, mat_a, ca, mat_b, cb, n_mats):
                def mat(c):
                    return m(c).unsqueeze(1).broadcast_to([96, n_mats, 96])

                def coef(c):
                    return c.unsqueeze(2).broadcast_to([96, n_mats, 96])

                chain(nc.gpsimd.tensor_tensor(dst[:, 0], mat(mat_a), coef(ca), ALU.mult))
                chain(nc.gpsimd.tensor_tensor(dst[:, 1], mat(mat_b), coef(cb), ALU.mult))
                settle()
                return nc.gpsimd.tensor_tensor(dst[:, 0], dst[:, 0], dst[:, 1], ALU.add)

            def second_input(H):
                yv = y2[:, H, :].rearrange("c (m b) -> c b m", b=T)
                for i in (0, 2):
                    pool.wait_ge(gl_ready, NT * H + i + 1)
                    nc.gpsimd.tensor_tensor(
                        yv[:, RT * i:RT * (i + 1), :], cols(gl, H, i).rearrange("c (b m) -> c b m", b=RT),
                        cols(fx, H, i).rearrange("c (b m) -> c b m", b=RT), ALU.add).then_inc(y2_pool, 1)

            def residual(H):
                for i in range(NT):
                    pool.wait_ge(fy_ready, NT * H + i + 1)
                    nc.gpsimd.tensor_tensor(
                        cols(res, H, i), cols(fy, H, i),
                        xs[:, HB * H + 2 * i:HB * H + 2 * i + 2, :].rearrange("c n l -> c (n l)"),
                        ALU.add).then_inc(res_ready, 1)

            pool.wait_ge(tables_ready, 1)
            combine(rotX, M_ID, tbl(XCO, NX), M_SW, tbl(XSI, NX), NX).then_inc(rotx_ready, 1)
            combine(yl, M_C, tbl(CU, T), M_CS, tbl(SU, T), T).then_inc(yl_ready, 1)
            for H in range(2):
                second_input(H)
                if H:
                    residual(0)
            residual(1)

        @block.scalar
        def _(act):
            act.dma_start(sm[:, :], small).then_inc(in_small, 16)
            act.dma_start(mt[:, 0:N_EARLY], mats[:, 0:N_EARLY]).then_inc(in_early, 16)
            act.dma_start(cmask[:, :], mask_in).then_inc(in_mask, 16)
            act.wait_ge(in_mask, 16)
            nc.scalar.activation(bcm[:, :, :], cmask[:, :].unsqueeze(2).broadcast_to([SR, NCH, 96]),
                                 ACT.Copy).then_inc(bcm_ready, 1)
            act.wait_ge(angles_ready, 1)
            nc.scalar.activation(tbl(SIN), tbl(RED), ACT.Sin).then_inc(sines_ready, 1)
            nc.scalar.activation(tbl(SH), tbl(RED), ACT.Sin, scale=0.5).then_inc(sines_ready, 1)

            def group_bias(H):
                act.wait_ge(bias_done, H + 1)
                nc.scalar.activation(gn[:, H, G_BIAS, 0:HB], bank(1, 2 * H + 1)[0:96, 2 * HB:3 * HB],
                                     ACT.Copy).then_inc(bias_ready, 1)

            def evacuate_batch(H, n, t, func, ready):
                act.wait_ge(centered[0], HB * H + 2 * (n // 2) + 2)
                if n == 0:
                    act.wait_ge(bias_ready, H + 1)
                nc.scalar.activation(
                    t[:, H, :].rearrange("c (b n a) -> c n b a", b=T, n=HB)[:, n],
                    bank(H, n // 2)[0:96, L * (n % 2):L * (n % 2 + 1)].rearrange("c (a b) -> c b a", b=T),
                    func, bias=gn[:, H, G_BIAS, n:n + 1]).then_inc(ready, 1)

            def centered_values(H, first, last):
                for n in range(first, last):
                    evacuate_batch(H, n, xc, ACT.Identity, taken[0])

            def squares(H, first, last):
                for n in range(first, last):
                    evacuate_batch(H, n, sq, ACT.Square, squared[0])

            def evacuate(H):
                act.wait_ge(vecs_ready, 1)
                for i in range(NT):
                    act.wait_ge(centered[1], NT * H + i + 1)
                    nc.scalar.activation(cols(sq, H, i), bank(H, i)[0:96, :], ACT.Square,
                                         bias=vecs[:, 2:3]).then_inc(squared[1], 1)
                    nc.scalar.activation(cols(xc, H, i), bank(H, i)[0:96, :], ACT.Identity,
                                         bias=vecs[:, 2:3]).then_inc(taken[1], 1)

            def first_state(H):
                act.wait_ge(u_done, NT * H + 1)
                nc.scalar.activation(rcols(w, H, 0), bank(H, 0)[0:96, 0:RC], ACT.Copy).then_inc(w_first, 1)

            def seed(H):
                act.wait_ge(z_sum, (1 + NDBL) * H + 1)
                nc.scalar.activation(
                    Z[:, H, :, 1:], bank(H, NT - 1)[0:96, 0:RC].rearrange("p (n a) -> p n a", a=NA)[:, :, 1:],
                    ACT.Copy).then_inc(z_seed, 1)

            def gelu_y(H):
                for i in range(NT):
                    act.wait_ge(y_done, NT * H + i + 1)
                    nc.scalar.activation(cols(gl, H, i), bank(H, i)[0:96, :], ACT.Gelu,
                                         bias=db[:, 0:1]).then_inc(gl_ready, 1)

            def gelu_z(H, i):
                act.wait_ge(enc_done, NT * H + i + 1)
                nc.scalar.activation(cols(gz, H, i), bank(*Z2[H, i])[0:96, :], ACT.Gelu,
                                     bias=vecs[:, 1:2]).then_inc(gz_ready, 1)

            group_bias(0)
            squares(0, 0, 2)
            centered_values(0, 0, 2)
            squares(0, 2, HB)
            centered_values(0, 2, HB)
            group_bias(1)
            squares(1, 0, 2)
            centered_values(1, 0, 2)
            squares(1, 2, 6)
            act.wait_ge(umat_done, 1)
            nc.scalar.activation(um[:, 0:5, :], bank(0, 2)[0:97, 0:480].rearrange("c (b j) -> c b j", j=96),
                                 ACT.Copy).then_inc(um_ready, 1)
            nc.scalar.activation(um[:, 5:8, :], bank(0, 3)[0:97, 0:288].rearrange("c (b j) -> c b j", j=96),
                                 ACT.Copy).then_inc(um_ready, 1)
            squares(1, 6, HB)
            centered_values(1, 2, HB)
            act.wait_ge(ones_ready, 2)
            first_state(0)
            act.wait_ge(vecs_done, 1)
            nc.scalar.activation(vecs[:, :], bank(1, 1)[0:96, 0:3], ACT.Copy).then_inc(vecs_ready, 1)
            seed(0)
            first_state(1)
            gelu_y(0)
            seed(1)
            evacuate(0)
            gelu_y(1)
            gelu_z(0, 0)
            evacuate(1)
            for i in range(1, NT):
                gelu_z(0, i)
            for i in range(NT):
                gelu_z(1, i)

        @block.tensor
        def _(pe):
            def mm(o, lhsT, rhs, start=True, stop=True):
                return nc.tensor.matmul(o, lhsT, rhs, start=start, stop=stop)

            def group_mean(H):
                pe.wait_ge(gn_stats, HB * (H + 1))
                mm(bank(1, 2 * H)[0:96, 0:2 * HB].rearrange("c (n e) -> c n e", e=2), m(M_NM),
                   st[:, HB * H:HB * (H + 1), 1:5:3]).then_inc(gn_mean, 1)

            def group_variance(H):
                var = bank(1, 2 * H + 1)[0:96, 0:2 * HB].rearrange("c (n e) -> c n e", e=2)
                mm(var, m(M_GV), st[:, HB * H:HB * (H + 1), 2:6:3], stop=False)
                pe.wait_ge(gn_dev, H + 1)
                mm(var, m(M_GD), gdev[:, H], start=False).then_inc(gn_var, 1)

            def group_bias(H):
                pe.wait_ge(gn_shift, H + 1)
                mm(bank(1, 2 * H + 1)[0:96, 2 * HB:3 * HB], m(M_P), gn[:, H, G_SHIFT, 0:HB]).then_inc(bias_done, 1)

            def warm_up(count, free):
                for _ in range(count):
                    mm(free[0:96, 0:96], m(M_P), m(M_P))

            def center_batch(H, n):
                pe.wait_ge(pm_ready, HB * H + n + 1)
                mm(bank(H, n // 2)[0:96, L * (n % 2):L * (n % 2 + 1)], pm[:, HB * H + n, :],
                   xs[:, HB * H + n, :]).then_inc(centered[0], 1)

            def center(H, i):
                mm(bank(H, i)[0:96, :], m(M_P), cols(y2, H, i)).then_inc(centered[1], 1)

            def variances(k, H, i):
                if i == 0:
                    pe.wait_ge(taken[k], NT * H + 1 if k else HB * H + 2)
                pe.wait_ge(squared[k], NT * H + i + 1 if k else HB * H + 2 * (i + 1))
                for j in range(NCH // NT):
                    r = NCH // NT * i + j if k else NT * j + i
                    last = mm(bank(H, 0)[0:NCH, 0:CH], m(M_Z + NCH - 1 - r, NCH), sq[:, H, CH * r:CH * (r + 1)],
                              start=(i + j == 0), stop=(i == NT - 1 and j == NCH // NT - 1))
                if i == NT - 1:
                    last.then_inc(variance[k], 1)

            def broadcast(k, H):
                pe.wait_ge(inv_ready[k], H + 1)
                for i in range(NT):
                    if k == 0:
                        pe.wait_ge(taken[0], HB * H + 2 * (i + 1))
                        if H == 0 and i >= 2:
                            pe.wait_ge(um_ready, i - 1)
                        if H == 1 and i == 1:
                            pe.wait_ge(vecs_ready, 1)
                    else:
                        pe.wait_ge(taken[1], NT * H + i + 1)
                    for j in range(TILE // CH):
                        last = mm(bank(H, i)[0:96, CH * j:CH * (j + 1)], bcm[:, TILE // CH * i + j, :], parts[:, H, :])
                    last.then_inc(inv_bcast[k], 1)

            def inputs(H, i):
                pe.wait_ge(fx_ready, NT * H + i + 1)
                for j in range(RT):
                    b = RT * i + j
                    last = mm(bank(H, i)[0:96, RC * j:RC * (j + 1)], um[:, b, :], rcols(fx, H, b, 97))
                last.then_inc(u_done, 1)

            def seed_sum(H):
                pe.wait_ge(w_local[H], T - 1)
                pe.wait_ge(rotx_ready, 1)
                w7 = rcols(w, H, T - 1).rearrange("p (n a) -> p n a", a=NA)
                o = bank(H, NT - 1)[0:96, 0:RC].rearrange("p (n a) -> p n a", a=NA)
                mm(o[:, :, 1:], rotX[:, 0, 0, :], w7[:, :, 0:NA - 1], stop=False)
                mm(o[:, :, 2:], rotX[:, 0, 1, :], w7[:, :, 0:NA - 2], start=False).then_inc(z_sum, 1)

            def doubling(H, k):
                d = 2 ** (k + 1)
                pe.wait_ge(z_seed, H + 1)
                if k:
                    pe.wait_ge(z_ready, NDBL * H + k)
                o = bank(H, NT - 1)[0:96, 0:RC].rearrange("p (n a) -> p n a", a=NA)
                mm(o[:, :, d:], rotX[:, 0, 2 + k, :], Z[:, H, :, 0:NA - d]).then_inc(z_sum, 1)

            def direct(H, i):
                if i < NT - 1:
                    pe.wait_ge(w_local[H], RT * (i + 1) - 1)
                else:
                    pe.wait_ge(z_ready, NDBL * (H + 1))
                mm(bank(H, i)[0:96, :], dm[:, :], cols(fx, H, i), stop=False)

            def outputs(H, i):
                for j in range(RT):
                    b = RT * i + j
                    pe.wait_ge(w_ready[H], b + 1)
                    last = mm(bank(H, i)[0:96, RC * j:RC * (j + 1)], yl[:, 0, b, :], rcols(w, H, b),
                              start=False, stop=(j == RT - 1))
                last.then_inc(y_done, 1)

            def encode(H, i):
                if H == 0:
                    pe.wait_ge(fy_ready, (2, 4, 4, 4)[i])
                    if i == 2:
                        pe.wait_ge(taken[1], NT + 3)
                    if i == 3:
                        pe.wait_ge(taken[1], 2 * NT)
                        pe.wait_ge(var_read, 4)
                else:
                    pe.wait_ge(fy_ready, NT + i + 1)
                    pe.wait_ge(out_ready, (1, 2, 3, 4)[i])
                mm(bank(*Z1[H, i])[0:96, :], m(M_WE), cols(fy, H, i))
                mm(bank(*Z2[H, i])[0:96, :], m(M_WE + 96), cols(fy, H, i)).then_inc(enc_done, 1)

            def decode(H, i):
                pe.wait_ge(zz_ready, NT * H + i + 1)
                mm(bank(*ZD[H, i])[0:96, :], m(M_WD), cols(zz, H, i)).then_inc(dec_done, 1)

            pe.wait_ge(in_early, 16)
            warm_up(WARM[0], bank(0, 3))
            group_mean(0)
            warm_up(WARM[1], bank(0, 3))
            group_variance(0)
            warm_up(WARM[2], bank(0, 3))
            center_batch(0, 0)
            center_batch(0, 1)
            group_bias(0)
            for n in range(2, HB):
                if n == 6:
                    group_mean(1)
                center_batch(0, n)
            group_variance(1)
            pe.wait_ge(in_mats, 16)
            for i in range(NT):
                variances(0, 0, i)
            center_batch(1, 0)
            group_bias(1)
            center_batch(1, 1)
            for i in range(1, NT):
                if i == NT - 1:
                    pe.wait_ge(bias_ready, 2)
                center_batch(1, 2 * i)
                center_batch(1, 2 * i + 1)
            variances(0, 1, 0)
            variances(0, 1, 1)
            pe.wait_ge(taken[0], HB)
            pe.wait_ge(bst_ready, 1)
            pe.wait_ge(rot_ready, T)
            mm(bank(0, 2)[0:97, 0:480], bst[:, :], rotT[:, 0:5, :])
            mm(bank(0, 3)[0:97, 0:288], bst[:, :], rotT[:, 5:8, :]).then_inc(umat_done, 1)
            pe.wait_ge(bcm_ready, 1)
            broadcast(0, 0)
            pe.wait_ge(ones_ready, 1)
            for i in range(NT):
                if i < 2:
                    variances(0, 1, i + 2)
                inputs(0, i)
            pe.wait_ge(taken[0], HB + 4)
            mm(bank(1, 1)[0:96, 0:1], m(M_WE), s(B2))
            mm(bank(1, 1)[0:96, 1:2], m(M_WE + 96), s(B2))
            mm(bank(1, 1)[0:96, 2:3], m(M_P), s(B1)).then_inc(vecs_done, 1)
            pe.wait_ge(dm_ready, 1)
            for i in range(NT - 1):
                direct(0, i)
            seed_sum(0)
            broadcast(0, 1)
            for i in range(NT):
                inputs(1, i)
                doubling(0, i)
            direct(0, NT - 1)
            pe.wait_ge(yl_ready, 1)
            for i in range(NT):
                outputs(0, i)
                if i < NT - 2:
                    direct(1, i)
            direct(1, NT - 2)
            seed_sum(1)
            pe.wait_ge(y2_pool, 2)
            pe.wait_ge(y2_vec, 2)
            for i in range(NT):
                center(0, i)
                doubling(1, i)
            for i in range(NT):
                variances(1, 0, i)
            direct(1, NT - 1)
            for i in range(NT):
                outputs(1, i)
            broadcast(1, 0)
            encode(0, 0)
            pe.wait_ge(y2_pool, 4)
            pe.wait_ge(y2_vec, 4)
            for i in range(NT):
                center(1, i)
            encode(0, 1)
            for i in range(NT):
                variances(1, 1, i)
            encode(0, 2)
            decode(0, 0)
            encode(0, 3)
            decode(0, 1)
            decode(0, 2)
            decode(0, 3)
            broadcast(1, 1)
            encode(1, 0)
            encode(1, 1)
            encode(1, 2)
            decode(1, 0)
            encode(1, 3)
            decode(1, 1)
            decode(1, 2)
            decode(1, 3)

        @block.vector
        def _(dve):
            def stt(o, a, sca, b, op0, op1):
                return nc.vector.scalar_tensor_tensor(out=o, in0=a, scalar=sca, in1=b, op0=op0, op1=op1)

            def scaled(o, a, s1, s2, op0, op1=None):
                if s2 is None:
                    return nc.vector.tensor_scalar(o, a, s1, None, op0)
                return nc.vector.tensor_scalar(o, a, s1, s2, op0, op1)

            class Steps:
                def __init__(self, done):
                    self.done, self.count = done, 0

                def add(self, ins):
                    self.count += 1
                    ins.then_inc(self.done, 1)

                def settle(self):
                    dve.wait_ge(self.done, self.count)

                def next_stt(self, *a):
                    self.settle()
                    self.add(stt(*a))

                def next_ts(self, *a):
                    self.settle()
                    self.add(scaled(*a))

                def next_tt(self, *a):
                    self.settle()
                    self.add(nc.vector.tensor_tensor(*a))

            norm, par = Steps(norm_steps), Steps(par_steps)

            def expm1(p, y, arg):
                par.next_ts(y, arg, 1 / 128, -80 / 128, ALU.mult, ALU.max)
                yield
                par.next_ts(p, y, 1 / 120, None, ALU.mult)
                yield
                for c in (1 / 24, 1 / 6, 1 / 2, 1.0):
                    par.next_stt(p, p, c, y, ALU.add, ALU.mult)
                    yield
                for _ in range(7):
                    par.next_stt(p, p, 2.0, p, ALU.add, ALU.mult)
                    yield

            def parameters():
                par.next_stt(scol(REC), s(LS), -1.0, s(LS), ALU.mult, ALU.max)
                yield
                yield from expm1(scol(EXP), scol(Y1), scol(REC))
                par.next_ts(scol(EXP1), scol(EXP), 1.0, None, ALU.add)
                par.add(scaled(scol(NEG), s(LS), 0.0, None, ALU.is_lt))
                par.add(scaled(scol(POS), s(LS), 0.0, None, ALU.is_ge))
                yield
                par.settle()
                par.add(nc.vector.reciprocal(scol(REC1), scol(EXP1)))
                yield
                par.next_tt(scol(T4), scol(REC1), scol(NEG), ALU.mult)
                yield
                par.next_stt(scol(STEP), scol(EXP1), scol(POS), scol(T4), ALU.mult, ALU.add)
                yield
                par.next_tt(scol(TH), s(LI), scol(STEP), ALU.mult)
                par.add(nc.vector.tensor_tensor(scol(RE), s(LR), scol(STEP), ALU.mult))
                yield
                par.next_ts(tbl(ANG), s(KV, NK), scol(TH), None, ALU.mult)
                par.add(scaled(tbl(XK), s(KV, NK), scol(RE), None, ALU.mult))
                yield
                par.next_ts(tbl(NRND), tbl(ANG), 1 / (2 * np.pi), ROUND, ALU.mult, ALU.add)
                yield
                par.next_ts(tbl(NRND), tbl(NRND), -ROUND, None, ALU.add)
                yield
                for part in (TWO_PI_HI, TWO_PI_MID, TWO_PI_LO):
                    par.next_stt(tbl(ANG), tbl(NRND), -float(part), tbl(ANG), ALU.mult, ALU.add)
                    yield
                par.settle()
                scaled(tbl(RED), tbl(ANG), PI_BELOW, -PI_BELOW, ALU.min, ALU.max).then_inc(angles_ready, 1)
                yield
                yield from expm1(tbl(EXM), tbl(TMP), tbl(XK))
                dve.wait_ge(sines_ready, 2)
                par.next_tt(tbl(SH2), tbl(SH), tbl(SH), ALU.mult)
                par.add(scaled(tbl(NSS), tbl(SIN), s(RHO), None, ALU.mult))
                par.add(scaled(tbl(RK), tbl(EXM), 1.0, None, ALU.add))
                yield
                par.next_ts(tbl(CM1), tbl(SH2), -2.0, None, ALU.mult)
                par.add(nc.vector.tensor_tensor(tbl(RSIN), tbl(RK), tbl(SIN), ALU.mult))
                par.add(nc.vector.tensor_tensor(scol(T2), s(LR), s(LR), ALU.mult))
                yield
                par.settle()
                scaled(tbl(COS), tbl(CM1), 1.0, None, ALU.add).then_inc(cos_ready, 1)
                par.add(nc.vector.tensor_tensor(scol(T3), tbl(RSIN, 1, 1), s(LI), ALU.mult))
                par.add(stt(scol(DEN), s(LI), s(LI), scol(T2), ALU.mult, ALU.add))
                yield
                dve.wait_ge(cos_ready, 1)
                par.next_tt(scol(T1), tbl(EXM, 1, 1), tbl(COS, 1, 1), ALU.mult)
                par.add(nc.vector.reciprocal(scol(DEN), scol(DEN)))
                yield
                par.next_tt(scol(T1), scol(T1), tbl(CM1, 1, 1), ALU.add)
                yield
                par.next_tt(scol(T4), scol(T1), s(LI), ALU.mult)
                par.add(stt(scol(CRE), scol(T1), s(LR), scol(T3), ALU.mult, ALU.add))
                yield
                par.next_stt(scol(CIM), tbl(RSIN, 1, 1), s(LR), scol(T4), ALU.mult, ALU.subtract)
                par.add(nc.vector.tensor_tensor(scol(CRE), scol(CRE), scol(DEN), ALU.mult))
                yield
                par.next_stt(scol(CIM), scol(CIM), scol(DEN), s(RHO), ALU.mult, ALU.mult)
                yield
                dve.wait_ge(in_mats, 16)
                par.next_ts(bt1[:, :], m(M_BS), scol(CIM), None, ALU.mult)
                yield
                par.next_stt(bst[:, 0:C], m(M_B), scol(CRE), bt1[:, :], ALU.mult, ALU.add)
                yield
                par.next_tt(bt1[:, :], bst[:, 0:C], m(M_B1), ALU.mult)
                yield
                par.settle()
                nc.vector.reduce_sum(bst[:, C:C + 1], bt1[:, :], axis=mybir.AxisListType.X).then_inc(bst_ready, 1)
                yield
                dve.wait_ge(rotcos_ready, 1)
                for b in range(T):
                    stt(rotT[:, b, :], m(M_SW), tbl(NSS, 1, b), rotT[:, b, :],
                        ALU.mult, ALU.add).then_inc(rot_ready, 1)
                    yield

            def output_tables():
                par.add(stt(scol(ABSI), s(LI), -1.0, s(LI), ALU.mult, ALU.max))
                par.add(scaled(tbl(SSG), tbl(SIN), s(NRHO), None, ALU.mult))
                yield
                par.next_tt(scol(ABSI), scol(ABSI), scol(STEP), ALU.mult)
                par.add(nc.vector.tensor_tensor(tbl(RSSG), tbl(RK), tbl(SSG), ALU.mult))
                yield
                par.next_ts(scol(MASK), scol(ABSI), float(np.float32(2 * np.pi)) / 4, 2.0, ALU.is_lt, ALU.mult)
                yield
                par.next_ts(scol(MR), scol(MASK), s(NRHO), None, ALU.mult)
                par.add(scaled(scol(MI), scol(MASK), -1.0, None, ALU.mult))
                yield
                par.next_ts(tbl(CU), tbl(COS), scol(MR), None, ALU.mult)
                par.add(scaled(tbl(SU), tbl(SIN), scol(MI), None, ALU.mult))
                yield
                for dst, unit in ((XCO, COS), (XSI, SSG)):
                    par.add(stt(tbl(dst, 1, 0), tbl(unit, 1, T), tbl(RK, 1, 1), tbl(RK, 1, 0),
                                ALU.mult, ALU.mult))
                    par.add(stt(tbl(dst, 1, 1), tbl(unit, 1, K16), tbl(RK, 1, 1), tbl(RK, 1, T),
                                ALU.mult, ALU.mult))
                    par.add(nc.vector.tensor_tensor(tbl(dst, 4, 2), tbl(unit, 4, K16), tbl(RK, 4, K16), ALU.mult))
                    yield
                par.settle()
                nc.vector.tensor_tensor(db[:, :], s(DD), s(B1), ALU.mult).then_inc(tables_ready, 1)
                yield
                scaled(dm[:, :], m(M_ID), s(DD), None, ALU.mult).then_inc(dm_ready, 1)
                yield

            input_steps, output_steps = parameters(), output_tables()

            def parameter_steps(count):
                for _ in range(count):
                    next(input_steps, None)

            def statistics(H, q):
                for k, (first, _) in enumerate(LOADS):
                    if first == HB * H + q:
                        dve.wait_ge(in_x[k], 16)
                nc.vector.bn_stats(st[:, HB * H + q, :], xs[:, HB * H + q, :]).then_inc(gn_stats, 1)

            def inverse_root(y, v, t, u, between=lambda j: None):
                norm.next_ts(y.bitcast(I32), v.bitcast(I32), -0.5, RSQRT_SEED, ALU.mult, ALU.add)
                between(0)
                norm.next_stt(t, y, -0.703952253, y, ALU.mult, ALU.mult)
                between(1)
                norm.next_tt(t, t, v, ALU.mult)
                between(2)
                norm.next_stt(y, t, 0.703952253 * 2.38924456, y, ALU.add, ALU.mult)
                between(3)
                norm.next_tt(t, y, y, ALU.mult)
                between(4)
                norm.next_tt(t, t, v, ALU.mult)
                between(5)
                norm.next_stt(u, t, -10 / 3, t, ALU.add, ALU.mult)
                between(6)
                norm.next_stt(y, u, 5.0, y, ALU.add, ALU.mult)

            def group_norm(H, between=lambda: None, after=lambda: None):
                var, t, u, minus, scale, shift = [gn[:, H, k, 0:HB] for k in
                                                (G_VAR, G_T, G_U, G_MINUS, G_SCALE, G_SHIFT)]
                dev = gdev[:, H]
                dve.wait_ge(gn_mean, H + 1)
                share = bank(1, 2 * H)[0:96, 0:2 * HB].rearrange("c (n e) -> c n e", e=2)
                norm.add(nc.vector.reduce_sum(minus, share, axis=mybir.AxisListType.X))
                between()
                norm.next_tt(dev, st[:, HB * H:HB * (H + 1), 1:5:3], minus.unsqueeze(2).broadcast_to([96, HB, 2]),
                             ALU.add)
                between()
                norm.settle()
                nc.vector.tensor_tensor(dev, dev, dev, ALU.mult).then_inc(gn_dev, 1)
                after()
                dve.wait_ge(gn_var, H + 1)
                share = bank(1, 2 * H + 1)[0:96, 0:2 * HB].rearrange("c (n e) -> c n e", e=2)
                norm.add(nc.vector.reduce_sum(u, share, axis=mybir.AxisListType.X))
                between()
                norm.next_ts(var, u, RSQRT_SCALE, RSQRT_SCALE * GN_EPS, ALU.mult, ALU.add)
                between()
                inverse_root(scale, var, t, u, lambda j: between() if H == 0 or j % 2 else None)
                norm.settle()
                nc.vector.tensor_tensor(shift, minus, scale, ALU.mult).then_inc(gn_shift, 1)

            def scale_centering(H, n):
                nc.vector.tensor_scalar(pm[:, HB * H + n, :], m(M_P), gn[:, H, G_SCALE, n:n + 1], None,
                                        ALU.mult).then_inc(pm_ready, 1)

            def inverse_sigma(k, H, between=lambda j: None):
                y, v, t, u = [rs[:, H, j, :] for j in range(4)]
                dve.wait_ge(variance[k], H + 1)
                scaled(v, bank(H, 0)[0:NCH, 0:CH], RSQRT_SCALE / C, RSQRT_SCALE * LN_EPS,
                       ALU.mult, ALU.add).then_inc(var_read, 1)
                dve.wait_ge(var_read, 2 * k + H + 1)
                between(-1)
                inverse_root(y, v, t, u, between)
                between(7)
                norm.next_ts(parts[0:NCH, H, :], y, 1.0, None, ALU.mult)
                between(8)
                norm.next_tt(t, y, parts[0:NCH, H, :], ALU.subtract)
                between(9)
                norm.next_ts(midc[:, H, :], t, 1.0, None, ALU.mult)
                norm.add(scaled(parts[NCH:2 * NCH, H, :], t, 1.0, None, ALU.mult))
                between(10)
                norm.settle()
                nc.vector.tensor_tensor(parts[2 * NCH:SR, H, :], t, midc[:, H, :],
                                        ALU.subtract).then_inc(inv_ready[k], 1)
                between(11)

            def scale_tile(k, H, i, dst, gain, ready):
                dve.wait_ge(inv_bcast[k], NT * H + i + 1)
                stt(cols(dst, H, i), cols(xc, H, i), gain, bank(H, i)[0:96, :],
                    ALU.mult, ALU.mult).then_inc(ready, 1)

            def scan(H, b):
                dve.wait_ge(u_done, NT * H + b // RT + 1)
                if b == 1:
                    dve.wait_ge(w_first, H + 1)
                else:
                    dve.wait_ge(w_local[H], b - 1)
                stt(rcols(w, H, b), rcols(w, H, b - 1), tbl(RK, 1, 1),
                    bank(H, b // RT)[0:96, RC * (b % RT):RC * (b % RT + 1)],
                    ALU.mult, ALU.add).then_inc(w_local[H], 1)

            def doubled(H, k):
                d = 2 ** (k + 1)
                dve.wait_ge(z_sum, (1 + NDBL) * H + k + 2)
                o = bank(H, NT - 1)[0:96, 0:RC].rearrange("p (n a) -> p n a", a=NA)
                zd = Z[:, H, :, d:]
                nc.vector.tensor_tensor(zd, zd, o[:, :, d:], ALU.add).then_inc(z_ready, 1)

            def carry(H, b):
                dve.wait_ge(z_ready, NDBL * (H + 1))
                stt(rcols(w, H, b), Z[:, H].rearrange("p n a -> p (n a)"), tbl(RK, 1, b), rcols(w, H, b),
                    ALU.mult, ALU.add).then_inc(w_ready[H], 1)

            def gate(H, i):
                dve.wait_ge(gz_ready, NT * H + i + 1)
                stt(cols(zz, H, i), bank(*Z1[H, i])[0:96, :], vecs[:, 0:1], cols(gz, H, i),
                    ALU.add, ALU.mult).then_inc(zz_ready, 1)

            def finish(H, i):
                dve.wait_ge(dec_done, NT * H + i + 1)
                dve.wait_ge(res_ready, NT * H + i + 1)
                stt(cols(ost, H, i), bank(*ZD[H, i])[0:96, :], s(B2), cols(res, H, i),
                    ALU.add, ALU.add).then_inc(out_ready, 1)

            dve.wait_ge(in_small, 16)
            parameter_steps(6)
            for q in range(HB):
                statistics(0, q)
                parameter_steps(1)
            dve.wait_ge(in_early, 16)
            statistics(1, 0)
            group_norm(0, lambda: parameter_steps(1), lambda: (statistics(1, 1), parameter_steps(2)))
            for n in range(HB):
                scale_centering(0, n)
                if n % 2:
                    parameter_steps(1)
            for q in range(2, HB):
                statistics(1, q)
                parameter_steps(1)
            parameter_steps(1)
            group_norm(1, lambda: parameter_steps(1), lambda: parameter_steps(2))
            for n in range(FIRST_PM):
                scale_centering(1, n)
                parameter_steps(1)
            inverse_sigma(0, 0, lambda j: scale_centering(1, FIRST_PM + 1 + j) if j < HB - FIRST_PM - 1
                          else parameter_steps(1))
            for _ in input_steps:
                pass
            for _ in output_steps:
                pass

            def second_input(H, i):
                dve.wait_ge(gl_ready, NT * H + i + 1)
                yv = y2[:, H, :].rearrange("c (m b) -> c b m", b=T)
                nc.vector.tensor_tensor(
                    yv[:, RT * i:RT * (i + 1), :], cols(gl, H, i).rearrange("c (b m) -> c b m", b=RT),
                    cols(fx, H, i).rearrange("c (b m) -> c b m", b=RT), ALU.add).then_inc(y2_vec, 1)

            for i in range(NT):
                scale_tile(0, 0, i, fx, s(G1), fx_ready)
            scan(0, 1)
            scan(0, 2)
            inverse_sigma(0, 1, lambda j: scan(0, j + 3) if 0 <= j < T - 3 else None)
            scale_tile(0, 1, 0, fx, s(G1), fx_ready)
            for i in range(NT):
                if i < NT - 1:
                    scale_tile(0, 1, i + 1, fx, s(G1), fx_ready)
                doubled(0, i)
            for b in range(T):
                carry(0, b)
                if b < T - 1:
                    scan(1, b + 1)
            second_input(0, 1)
            second_input(0, 3)
            for k in range(NDBL):
                doubled(1, k)
            for b in range(T - 1):
                carry(1, b)
            inverse_sigma(1, 0, lambda j: carry(1, T - 1) if j == -1 else None)
            second_input(1, 1)
            for i in range(NT):
                if i == 2:
                    second_input(1, 3)
                scale_tile(1, 0, i, fy, s(G2), fy_ready)
            dve.wait_ge(vecs_ready, 1)
            gate(0, 0)
            gate(0, 1)
            inverse_sigma(1, 1, lambda j: gate(0, 2) if j == 7 else None)
            gate(0, 3)
            finish(0, 0)
            finish(0, 1)
            scale_tile(1, 1, 0, fy, s(G2), fy_ready)
            finish(0, 2)
            scale_tile(1, 1, 1, fy, s(G2), fy_ready)
            finish(0, 3)
            scale_tile(1, 1, 2, fy, s(G2), fy_ready)
            scale_tile(1, 1, 3, fy, s(G2), fy_ready)
            gate(1, 0)
            gate(1, 1)
            gate(1, 2)
            finish(1, 0)
            gate(1, 3)
            finish(1, 1)
            finish(1, 2)
            finish(1, 3)


def mode_rows(a):
    return np.concatenate([a, a])


def constants():
    eye = np.eye(96, dtype=np.float32)
    groups = np.kron(np.eye(96 // GROUP), np.ones((GROUP, GROUP))).astype(np.float32)
    swap = np.roll(eye, 48, axis=1)
    rho = np.repeat(np.array([-1.0, 1.0], np.float32), 48)
    z = np.zeros((96, ZW), np.float32)
    z[:, NCH - 1] = 1.0
    mask = np.zeros((SR, NCH), np.float32)
    mask[np.arange(SR), np.arange(SR) % NCH] = 1.0
    return (-groups / np.float32(2 * GROUP), groups * np.float32(L / 2 / NGRP), groups / np.float32(NGRP),
            eye - np.float32(1.0 / C), eye, swap, z, rho, mask)


def kernel(x, L0_conv_ln1_g, L0_conv_ln1_b, L0_conv_Lambda, L0_conv_Bmat, L0_conv_Cmat, L0_conv_D,
           L0_conv_log_step, L0_conv_ln2_g, L0_conv_ln2_b, L0_conv_W_enc, L0_conv_W_dec):
    import concourse.bacc as bacc
    from concourse.bass_utils import run_bass_kernel_spmd

    f = [np.ascontiguousarray(a) for a in (x, L0_conv_ln1_g, L0_conv_ln1_b, L0_conv_Lambda, L0_conv_Bmat,
                                           L0_conv_Cmat, L0_conv_D, L0_conv_log_step, L0_conv_ln2_g,
                                           L0_conv_ln2_b, L0_conv_W_enc, L0_conv_W_dec)]
    x, g1, b1, lam, bm, cm, dd, ls, g2, b2, we, wd = f
    minus_mean, means_weight, var_weight, center, eye, swap, z, rho, mask = constants()
    powers = np.tile(np.array(POWERS, np.float32), (96, 1))
    small = np.concatenate(
        [np.stack([mode_rows(lam[:, 0]), mode_rows(lam[:, 1]), mode_rows(ls), rho, -rho, g1, b1, dd, g2, b2], 1),
         powers], 1)
    b_own = np.concatenate([bm[:, :, 0], bm[:, :, 1]])
    b_swapped = np.concatenate([bm[:, :, 1], bm[:, :, 0]])
    c_own = np.concatenate([cm[:, :, 0].T, cm[:, :, 1].T])
    c_swapped = np.concatenate([cm[:, :, 1].T, cm[:, :, 0].T])
    mats = np.concatenate([minus_mean, means_weight, var_weight, center, eye, swap, b_own, b_swapped, c_own, c_swapped,
                           np.tile(b1, (96, 1)), wd.T, we.T, z], 1)
    arrays = {
        "x_dram": x.reshape(B, C, L),
        "small_dram": np.ascontiguousarray(small),
        "mats_dram": np.ascontiguousarray(mats),
        "mask_dram": mask,
    }
    nc = bacc.Bacc("TRN2", target_bir_lowering=False, num_devices=1)
    aps = {k: nc.dram_tensor(k, a.shape, mybir.dt.from_np(a.dtype), kind="ExternalInput").ap()
           for k, a in arrays.items()}
    out = nc.dram_tensor("out_dram", (B, C, L), F32, kind="ExternalOutput").ap()
    s5_block(nc, aps["x_dram"].rearrange("n c l -> c n l"), aps["small_dram"], aps["mats_dram"], aps["mask_dram"],
             out.rearrange("n c l -> c n l"))
    r = run_bass_kernel_spmd(nc, [arrays], core_ids=[0])
    return r.results[0]["out_dram"].reshape(B, C, 16, 16)
```
